# Optimizing a Trainium2 kernel written in Bass

```python
import numpy as np
import jax
import jax.numpy as jnp

def _softmax(x, axis=-1):
    return jax.nn.softmax(x, axis=axis)

def _gelu(x):
    return jax.nn.gelu(x, approximate=True)

def _silu(x):
    return jax.nn.silu(x)

def _sigmoid(x):
    return jax.nn.sigmoid(x)

def _layernorm(x, axis=-1, eps=1e-05):
    m = jnp.mean(x, axis=axis, keepdims=True)
    v = jnp.var(x, axis=axis, keepdims=True)
    return (x - m) / jnp.sqrt(v + eps)

def _scatter_add(tgt, idx, src, axis=0):
    return tgt.at[idx].add(src)

def _segment_sum(src, seg, n):
    return jax.ops.segment_sum(src, seg, n)
kernel_name = 'mk_seq_postln_d1_jaxref_r4_1978d0'

def setup_inputs(seed: int=0):
    np.random.seed(seed)
    _w = jnp.asarray

    def _L0_attn_setup():
        import jax, jax.numpy as jnp
        import numpy as np
        import math
        B, S, DM, H = (4, 1024, 256, 16)
        HD = DM // H
        key = jax.random.key(seed)
        ks = jax.random.split(key, 5)

        def xavier(k, shape):
            bound = math.sqrt(6.0 / (shape[0] + shape[1]))
            return jax.random.uniform(k, shape, jnp.float32, -bound, bound)
        return {'x': jax.random.normal(ks[0], (B, S, DM), jnp.float32), 'Wq': xavier(ks[1], (DM, DM)), 'Wk': xavier(ks[2], (DM, DM)), 'Wv': xavier(ks[3], (DM, DM)), 'Wfc': xavier(ks[4], (DM, DM))}
    _L0_attn_in = _L0_attn_setup()

    def _L0_ffn_setup():
        import jax, jax.numpy as jnp
        import numpy as np
        from jax import lax
        B, S, H = (2, 256, 256)
        I = 128
        E = 32
        TOP_K = 4
        N_GROUP = 4
        TOPK_GROUP = 2
        SCALE = 2.5
        N_SHARED = 2
        SH_I = I * N_SHARED

        def _route(tokens, router_weight, router_bias):
            logits = tokens.astype(jnp.float32) @ router_weight.astype(jnp.float32).T
            scores = jax.nn.sigmoid(logits)
            sfc = scores + router_bias[None, :]
            T = tokens.shape[0]
            grp = sfc.reshape(T, N_GROUP, E // N_GROUP)
            group_scores = lax.top_k(grp, 2)[0].sum(-1)
            _, gidx = lax.top_k(group_scores, TOPK_GROUP)
            gmask = jax.nn.one_hot(gidx, N_GROUP, dtype=sfc.dtype).sum(1)
            smask = jnp.broadcast_to(gmask[:, :, None], (T, N_GROUP, E // N_GROUP)).reshape(T, E)
            tmp = jnp.where(smask > 0, sfc, 0.0)
            _, topk_idx = lax.top_k(tmp, TOP_K)
            topk_w = jnp.take_along_axis(scores, topk_idx, axis=1)
            topk_w = topk_w / (topk_w.sum(-1, keepdims=True) + 1e-20)
            topk_w = topk_w * SCALE
            return (topk_idx, topk_w)
        key = jax.random.key(seed)
        ks = jax.random.split(key, 10)
        std = 0.02
        return {'hidden_states': jax.random.normal(ks[0], (B, S, H), jnp.float32), 'router_weight': jax.random.normal(ks[1], (E, H), jnp.float32) * std, 'router_bias': jnp.zeros((E,), jnp.float32), 'gate_w': jax.random.normal(ks[2], (E, I, H), jnp.float32) * std, 'up_w': jax.random.normal(ks[3], (E, I, H), jnp.float32) * std, 'down_w': jax.random.normal(ks[4], (E, H, I), jnp.float32) * std, 'shared_gate_w': jax.random.normal(ks[5], (SH_I, H), jnp.float32) * std, 'shared_up_w': jax.random.normal(ks[6], (SH_I, H), jnp.float32) * std, 'shared_down_w': jax.random.normal(ks[7], (H, SH_I), jnp.float32) * std}
    _L0_ffn_in = _L0_ffn_setup()
    _d = {'L0_attn_x': _L0_attn_in['x'], 'L0_attn_Wq': _L0_attn_in['Wq'], 'L0_attn_Wk': _L0_attn_in['Wk'], 'L0_attn_Wv': _L0_attn_in['Wv'], 'L0_attn_Wfc': _L0_attn_in['Wfc'], 'L0_ffn_router_weight': _L0_ffn_in['router_weight'], 'L0_ffn_router_bias': _L0_ffn_in['router_bias'], 'L0_ffn_gate_w': _L0_ffn_in['gate_w'], 'L0_ffn_up_w': _L0_ffn_in['up_w'], 'L0_ffn_down_w': _L0_ffn_in['down_w'], 'L0_ffn_shared_gate_w': _L0_ffn_in['shared_gate_w'], 'L0_ffn_shared_up_w': _L0_ffn_in['shared_up_w'], 'L0_ffn_shared_down_w': _L0_ffn_in['shared_down_w']}
    _x0 = _d['L0_attn_x']
    _d['L0_attn_x'] = jax.random.normal(jax.random.fold_in(jax.random.key(seed), 1), (4, 1024, 256), dtype=_x0.dtype)
    del _x0
    return _d

def reference(L0_attn_x, L0_attn_Wq, L0_attn_Wk, L0_attn_Wv, L0_attn_Wfc, L0_ffn_router_weight, L0_ffn_router_bias, L0_ffn_gate_w, L0_ffn_up_w, L0_ffn_down_w, L0_ffn_shared_gate_w, L0_ffn_shared_up_w, L0_ffn_shared_down_w):

    def _L0_attn_ref(x, Wq, Wk, Wv, Wfc):
        import jax, jax.numpy as jnp
        import numpy as np
        import math
        B, S, DM, H = (4, 1024, 256, 16)
        HD = DM // H
        b, s, dm = x.shape
        h, hd = (H, dm // H)
        Q = (x @ Wq.T).reshape(b, s, h, hd)
        K = (x @ Wk.T).reshape(b, s, h, hd)
        V = (x @ Wv.T).reshape(b, s, h, hd)
        scores = jnp.einsum('bshd,bstd->bsht', Q, K) / math.sqrt(hd)
        attn = jax.nn.softmax(scores, axis=-1)
        out = jnp.einsum('bsht,bstd->bshd', attn, V).reshape(b, s, dm)
        return out @ Wfc.T

    def _L0_ffn_ref(hidden_states, router_weight, router_bias, gate_w, up_w, down_w, shared_gate_w, shared_up_w, shared_down_w):
        import jax, jax.numpy as jnp
        import numpy as np
        from jax import lax
        B, S, H = (2, 256, 256)
        I = 128
        E = 32
        TOP_K = 4
        N_GROUP = 4
        TOPK_GROUP = 2
        SCALE = 2.5
        N_SHARED = 2
        SH_I = I * N_SHARED

        def _route(tokens, router_weight, router_bias):
            logits = tokens.astype(jnp.float32) @ router_weight.astype(jnp.float32).T
            scores = jax.nn.sigmoid(logits)
            sfc = scores + router_bias[None, :]
            T = tokens.shape[0]
            grp = sfc.reshape(T, N_GROUP, E // N_GROUP)
            group_scores = lax.top_k(grp, 2)[0].sum(-1)
            _, gidx = lax.top_k(group_scores, TOPK_GROUP)
            gmask = jax.nn.one_hot(gidx, N_GROUP, dtype=sfc.dtype).sum(1)
            smask = jnp.broadcast_to(gmask[:, :, None], (T, N_GROUP, E // N_GROUP)).reshape(T, E)
            tmp = jnp.where(smask > 0, sfc, 0.0)
            _, topk_idx = lax.top_k(tmp, TOP_K)
            topk_w = jnp.take_along_axis(scores, topk_idx, axis=1)
            topk_w = topk_w / (topk_w.sum(-1, keepdims=True) + 1e-20)
            topk_w = topk_w * SCALE
            return (topk_idx, topk_w)
        tokens = hidden_states.reshape(-1, H)
        topk_idx, topk_w = _route(tokens, router_weight, router_bias)
        gate_vals = jax.nn.silu(jnp.einsum('th,eih->tei', tokens, gate_w))
        up_vals = jnp.einsum('th,eih->tei', tokens, up_w)
        hidden_vals = gate_vals * up_vals
        expert_out = jnp.einsum('tei,ehi->teh', hidden_vals, down_w)
        sel = jnp.take_along_axis(expert_out, topk_idx[:, :, None], axis=1)
        mixed = (sel * topk_w[:, :, None].astype(sel.dtype)).sum(1)
        mixed = mixed.reshape(hidden_states.shape)
        sg = jax.nn.silu(jnp.einsum('bsh,ih->bsi', hidden_states, shared_gate_w))
        su = jnp.einsum('bsh,ih->bsi', hidden_states, shared_up_w)
        shared = jnp.einsum('bsi,hi->bsh', sg * su, shared_down_w)
        return mixed + shared
    x = L0_attn_x
    x = _layernorm(x + _L0_attn_ref(x, L0_attn_Wq, L0_attn_Wk, L0_attn_Wv, L0_attn_Wfc), axis=-1)
    x = _layernorm(x + _L0_ffn_ref(x, L0_ffn_router_weight, L0_ffn_router_bias, L0_ffn_gate_w, L0_ffn_up_w, L0_ffn_down_w, L0_ffn_shared_gate_w, L0_ffn_shared_up_w, L0_ffn_shared_down_w), axis=-1)
    return x

_drawn_inputs = setup_inputs


def setup_inputs(seed=0):
    import zlib

    import numpy as np

    out = dict(_drawn_inputs(seed))
    spreads = {'L0_ffn_router_bias': (0.0, 0.51)}
    factors = {'L0_ffn_router_weight': 4.564,
     'L0_ffn_gate_w': 3.824,
     'L0_ffn_up_w': 3.778,
     'L0_ffn_down_w': 3.778,
     'L0_ffn_shared_gate_w': 3.405,
     'L0_ffn_shared_up_w': 3.363,
     'L0_ffn_shared_down_w': 3.368}
    for name, (base, spread) in spreads.items():
        noise = np.random.default_rng([zlib.crc32(name.encode()), seed]).standard_normal(out[name].shape)
        drawn = base * np.exp(spread * noise) if base else spread * noise
        out[name] = jnp.asarray(drawn.astype(out[name].dtype))
    for name, factor in factors.items():
        out[name] = (out[name] * factor).astype(out[name].dtype)
    return out
```

```python
from contextlib import ExitStack

import concourse.bass as bass
from concourse import mybir

F32 = mybir.dt.float32
BF16 = mybir.dt.bfloat16
U32 = mybir.dt.uint32
I32 = mybir.dt.int32
ALU = mybir.AluOpType
ACT = mybir.ActivationFunctionType
AX = mybir.AxisListType.X

P = 128
NTOK, DM = 4096, 256
NT = NTOK // P
KC = DM // P
NH = 16
HD = DM // NH
NE, EI = 32, 128
TOPK, NGROUP = 4, 4
GSZ = NE // NGROUP
SHI = 256
SCALE = 2.5
EPS = 1e-5
ROW = DM + 8
ID, WT = DM, DM + 1
QUAD = 4
MAXTILES = NTOK * TOPK // P + NE - 1
SLOTS = 2 * P
REGION = NTOK + P
XROWS = NE * REGION + QUAD * P
NOWHERE = 1 << 18
assert MAXTILES + QUAD <= SLOTS


class Tile:

    def __init__(self, pair, par):
        self.pair, self.par, self.n = pair, par, pair * 2 + par

    def ago(self, k):
        q = self.par - k
        return Tile(self.pair + q // 2, q % 2)

    @property
    def exists(self):
        return not isinstance(self.n, int) or 0 <= self.n < NT

    def since(self, k):
        return not isinstance(self.n, int) or self.n >= k


def each_step(eng, first, last, lead, lag, body):
    lo = lag + lag % 2 + 2
    hi = (NT - lead) // 2 * 2
    for s in range(first, lo):
        body(Tile(s // 2, s % 2))
    with eng.Fori(lo // 2, hi // 2) as pair:
        body(Tile(pair, 0))
        body(Tile(pair, 1))
    for s in range(hi, last + 1):
        body(Tile(s // 2, s % 2))


def build(nc, xT, x, wqkv, wfc, wr, rbias, wsgu, wsd, wgu, wd, out):
    xs = nc.dram_tensor("expert_rows", [XROWS, ROW], F32).ap()
    z = nc.dram_tensor("pick_rows", [TOPK * NTOK, DM], F32).ap()

    with ExitStack() as ctx:
        def sb(name, shape, dt=F32):
            return ctx.enter_context(nc.sbuf_tensor(name, shape, dt))

        def bank(name):
            return ctx.enter_context(nc.psum_tensor(name, [P, 512], F32))

        def sem(name):
            return ctx.enter_context(nc.semaphore(name))

        wqkv_sb = sb("wqkv_sb", [P, KC, 3 * DM])
        wfc_sb = sb("wfc_sb", [P, KC, DM])
        wr_sb = sb("wr_sb", [P, KC, NE])
        bias_sb = sb("bias_sb", [P, NE])
        wsgu_sb = sb("wsgu_sb", [P, KC, 2 * SHI])
        wsd_sb = sb("wsd_sb", [P, SHI // P, DM])
        wgu_sb = sb("wgu_sb", [P, NE * KC * 2 * EI])
        wd_sb = sb("wd_sb", [P, NE * DM])
        ident = sb("ident", [P, P])
        ones_b = sb("ones_b", [P, P], BF16)
        before_b = sb("before_b", [P, P], BF16)
        iota_e = sb("iota_e", [P, NE])
        slot_col = sb("slot_col", [P, 2])
        neg_half = sb("neg_half", [P, 1])
        pad_rows = sb("pad_rows", [P, ROW])
        xT_sb = [sb(f"xT_sb{i}", [P, KC, P]) for i in range(2)]
        x_sb = [sb(f"x_sb{i}", [P, DM]) for i in range(2)]
        kv_sb = [sb(f"kv_sb{i}", [P, 2 * DM]) for i in range(2)]
        prod = sb("prod", [P, NH * NH * HD])
        scores = sb("scores", [P, NH * NH])
        smax = sb("smax", [P, NH])
        shifted = sb("shifted", [P, NH * NH])
        psum_row = sb("psum_row", [P, NH])
        prec = sb("prec", [P, NH])
        att = sb("att", [P, DM])
        o_sb = sb("o_sb", [P, DM])
        oT_sb = sb("oT_sb", [P, KC, P])
        res = sb("res", [P, DM])
        stats = sb("stats", [P, 6])
        mv = [sb(f"mv{i}", [P, 2]) for i in range(2)]
        veps = [sb(f"veps{i}", [P, 1]) for i in range(2)]
        rstd = [sb(f"rstd{i}", [P, 1]) for i in range(2)]
        x1 = [sb(f"x1_{i}", [P, DM]) for i in range(2)]
        x1T_sb = sb("x1T_sb", [P, KC, P])
        th_sb = sb("th_sb", [P, SHI])
        gth_sb = sb("gth_sb", [P, SHI])
        hs_sb = sb("hs_sb", [P, SHI])
        hsT_sb = sb("hsT_sb", [P, SHI // P, P])
        sx = sb("sx", [P, NT * DM])
        eneg = sb("eneg", [P, NE])
        eneg1 = sb("eneg1", [P, NE])
        sig = sb("sig", [P, NE])
        sfc = sb("sfc", [P, NE])
        gtop = sb("gtop", [P, NGROUP, 8])
        gscore = sb("gscore", [P, 8])
        gbest = sb("gbest", [P, 8])
        gidx = sb("gidx", [P, 8], U32)
        gidxf = sb("gidxf", [P, 8])
        gmask0 = sb("gmask0", [P, NGROUP])
        gmask = sb("gmask", [P, NGROUP])
        masked = sb("masked", [P, NE])
        best = sb("best", [P, 8])
        bidx = sb("bidx", [P, 8], U32)
        bidxf = sb("bidxf", [P, 8])
        onehot = sb("onehot", [P, TOPK, NE])
        wsel = sb("wsel", [P, TOPK, NE])
        w4 = sb("w4", [P, TOPK])
        wsum = sb("wsum", [P, 1])
        wsum1 = sb("wsum1", [P, 1])
        wrec = sb("wrec", [P, 1])
        picks = [sb(f"picks{i}", [P, NE], BF16) for i in range(2)]
        seen = [sb(f"seen{i}", [P, NE], BF16) for i in range(2)]
        rsel = sb("rsel", [P, TOPK, NE])
        rank = sb("rank", [P, TOPK])
        pos = [sb(f"pos{i}", [P, TOPK], U32) for i in range(2)]
        outid = sb("outid", [P, TOPK], U32)
        stage = [sb(f"stage{i}", [P, TOPK, ROW]) for i in range(2)]
        cnt_u = sb("cnt_u", [P, NE], U32)
        ntile_u = sb("ntile_u", [P, NE], U32)
        ntile = sb("ntile", [P, NE])
        ones_e = sb("ones_e", [P, NE])
        tend = sb("tend", [P, NE])
        past = sb("past", [P, 2, NE])
        pend = sb("pend", [P, 2, NE])
        slot_e = sb("slot_e", [P, 2])
        slot_first = sb("slot_first", [P, 2])
        slot_k = sb("slot_k", [P, 2])
        slot_row = sb("slot_row", [P, 4])
        region0 = sb("region0", [P, NE])
        tab = sb("tab", [1, 2 * SLOTS + NE + 8], I32)
        quadf = sb("quadf", [P, 1], U32)
        xt = [sb(f"xt{i}", [P, 2, ROW]) for i in range(2)]
        meta = [sb(f"meta{i}", [P, 2, 2]) for i in range(2)]
        cth = [sb(f"cth{i}", [P, 2, EI]) for i in range(2)]
        cgth = sb("cgth", [P, 2, EI])
        ch = sb("ch", [P, 2, EI])
        def over_prod(at, *shape):
            size = 1
            for s in shape:
                size *= s
            part = prod[:, at:at + size]
            return part.rearrange("p (a b) -> p a b", a=shape[0]) if len(shape) > 1 else part

        xtT = over_prod(0, 2 * KC * P)
        chT = over_prod(2 * DM, 2 * P)
        y_sb = [over_prod((4 + 2 * i) * DM, 2, DM) for i in range(2)]
        zt = [over_prod(i * TOPK * DM, TOPK, DM) for i in range(2)]
        z2 = over_prod(8 * DM, 2, DM)
        z1 = over_prod(10 * DM, DM)
        zr = [over_prod((11 + i) * DM, DM) for i in range(2)]
        o2 = [over_prod((13 + i) * DM, DM) for i in range(2)]

        banks = [bank(f"bank{i}") for i in range(8)]
        q_ps = banks[0:2]
        kv_ps = banks[2]
        tr_ps = banks[3]
        y_ps = banks[4]
        gu_ps = banks[5]
        att_ps = banks[6]
        misc_ps = banks[7]

        SEMS = """x_loaded0 x_loaded1 small_w big_w consts pads cast
        qkv_ready kv_copied qk_prod qk_sum qk_max qk_shift p_ready p_sum p_rec pv_prod pv_sum att_ready
        oT_ps oT_copied y_ready res_ready st_ready mv_ready veps_ready rstd_ready x1_ready staged
        x1T_ps x1T_copied logits_ready gu_ready eneg_ready th_ready gth_ready hs_ready hsT_ps hsT_copied
        sd_ready sx_ready route picks_ready rank_ready rk pos_ready scat0 scat1
        count_ready b tabT tab_ready filled
        xt0 xt1 cX_ps cX_copied cmeta cgu_ps cth_ready cgth_ready ch_ready chT_ps chT_copied cy_ps cy_copied
        yscat0 yscat1
        z_loaded0 z_loaded1 d_a d_b zr_ready dst_ready dmv_ready dveps_ready drstd_ready o2_ready
        stored0 stored1""".split()
        S = {name: sem(name) for name in SEMS}
        x_loaded = [S["x_loaded0"], S["x_loaded1"]]
        scattered = [S["scat0"], S["scat1"]]
        xt_loaded = [S["xt0"], S["xt1"]]
        y_scattered = [S["yscat0"], S["yscat1"]]
        z_loaded = [S["z_loaded0"], S["z_loaded1"]]
        stored = [S["stored0"], S["stored1"]]

        NSMALL = 6 * 16
        QUADS = 2 * SLOTS + NE

        block = ctx.enter_context(nc.Block())

        def wait_apart(eng, semaphore, value):
            goal = value if isinstance(value, int) else eng.snap(eng.to_reg(value))
            eng.wait_ge(S["consts"], 12)
            eng.wait_ge(semaphore, goal)

        def n_quads(eng):
            eng.wait_ge(S["tab_ready"], 1)
            return eng.value_load(tab[0:1, QUADS:QUADS + 1], min_val=NTOK * TOPK // P // QUAD - 2,
                                  max_val=(MAXTILES + QUAD - 1) // QUAD - 2) + 2

        @block.sync
        def _(sp):
            sp.dma_start(wqkv_sb[:, :, :], wqkv).then_inc(S["small_w"], 16)

            def load_x(t):
                if t.since(2):
                    sp.wait_ge(S["res_ready"], t.n - 1)
                sp.dma_start(xT_sb[t.par][:, :, :], xT[bass.ds(t.n * P, P), :]).then_inc(x_loaded[t.par], 16)
                sp.dma_start(x_sb[t.par][:, :], x[bass.ds(t.n * P, P), :]).then_inc(x_loaded[t.par], 16)

            load_x(Tile(0, 0))
            load_x(Tile(0, 1))
            for dst, src in ((wfc_sb[:, :, :], wfc), (wr_sb[:, :, :], wr), (wsgu_sb[:, :, :], wsgu),
                             (wsd_sb[:, :, :], wsd), (bias_sb[:, :], rbias)):
                sp.dma_start(dst, src).then_inc(S["small_w"], 16)
            with sp.Fori(1, NT // 2) as pair:
                load_x(Tile(pair, 0))
                load_x(Tile(pair, 1))

            quads = n_quads(sp)
            for par in range(2):
                sp.wait_ge(scattered[par], 16 * TOPK * (NT // 2))
            sp.wait_ge(S["filled"], 16 * NE)
            sp.wait_ge(S["pads"], 16 * QUAD)

            def load_rows(pair, par, first):
                if not first:
                    sp.wait_ge(S["cX_ps"], 2 * pair + par - 1)
                    sp.wait_ge(S["cmeta"], 2 * pair + par - 1)
                for j in range(2):
                    row = sp.value_load(tab[0:1, bass.ds(pair * QUAD + 2 * par + j, 1)],
                                        min_val=0, max_val=XROWS - P)
                    sp.dma_start(xt[par][:, j, :], xs[bass.ds(row, P), :]).then_inc(xt_loaded[par], 16)

            load_rows(0, 0, True)
            load_rows(0, 1, True)
            with sp.Fori(1, quads) as quad:
                load_rows(quad, 0, False)
                load_rows(quad, 1, False)

            for par in range(2):
                sp.wait_ge(y_scattered[par], quads * 32)

            def load_z(t):
                if t.since(2):
                    sp.wait_ge(S["d_a"], t.n - 1)
                sp.dma_start(zt[t.par][:, :, :],
                             z.rearrange("(k n) c -> n k c", k=TOPK)[bass.ds(t.n * P, P), :, :])\
                    .then_inc(z_loaded[t.par], 16)

            load_z(Tile(0, 0))
            load_z(Tile(0, 1))
            with sp.Fori(1, NT // 2) as pair:
                load_z(Tile(pair, 0))
                load_z(Tile(pair, 1))

        @block.gpsimd
        def _(pool):
            pool.memset(ident[:, :], 1.0).then_inc(S["consts"], 1)
            pool.memset(before_b[:, :], 1.0).then_inc(S["consts"], 1)
            pool.memset(ones_b[:, :], 1.0).then_inc(S["consts"], 1)
            pool.memset(neg_half[:, :], -0.5).then_inc(S["consts"], 1)
            pool.memset(pad_rows[:, :], 0.0).then_inc(S["consts"], 1)
            pool.iota(iota_e[:, :], [[1, NE]], base=0, channel_multiplier=0,
                      allow_small_or_imprecise_dtypes=True).then_inc(S["consts"], 1)
            pool.iota(slot_col[:, :], [[P, 2]], base=0, channel_multiplier=1,
                      allow_small_or_imprecise_dtypes=True).then_inc(S["consts"], 1)
            pool.iota(region0[:, :], [[REGION, NE]], base=0, channel_multiplier=0,
                      allow_small_or_imprecise_dtypes=True).then_inc(S["consts"], 1)
            pool.iota(outid[:, :], [[NTOK, TOPK]], base=0, channel_multiplier=1).then_inc(S["consts"], 1)
            pool.wait_ge(S["consts"], 9)
            pool.affine_select(out=ident[:, :], in_=ident[:, :], compare_op=ALU.is_equal, fill=0.0,
                               base=0, pattern=[[-1, P]], channel_multiplier=1).then_inc(S["consts"], 1)
            pool.affine_select(out=before_b[:, :], in_=before_b[:, :], compare_op=ALU.is_gt, fill=0.0,
                               base=0, pattern=[[1, P]], channel_multiplier=-1).then_inc(S["consts"], 1)
            pool.iota(pad_rows[:, ID:ID + 1].bitcast(U32), [[0, 1]], base=NOWHERE,
                      channel_multiplier=0).then_inc(S["consts"], 1)

            def step(t):
                a, b = t.ago(1), t.ago(2)
                if a.exists:
                    pool.wait_ge(S["veps_ready"], a.n + 1)
                    pool.tensor_tensor(rstd[a.par][:, :], veps[a.par][:, :], neg_half[:, :], ALU.pow)\
                        .then_inc(S["rstd_ready"], 1)
                if b.exists:
                    wait_apart(pool, S["pos_ready"], b.n + 1)
                    wait_apart(pool, S["staged"], b.n + 1)
                    for k in range(TOPK):
                        pool.indirect_dma_start(
                            xs, bass.IndirectOffsetOnAxis(ap=pos[b.par][:, k:k + 1], axis=0),
                            stage[b.par][:, k, :], None, bounds_check=XROWS - 1,
                            oob_is_err=False).then_inc(scattered[b.par], 16)

            each_step(pool, 0, NT + 1, 0, 2, step)

            quads = n_quads(pool)

            def scatter_y(pair, par):
                wait_apart(pool, S["cy_copied"], pair * 2 + par + 1)
                for j in range(2):
                    pool.indirect_dma_start(
                        z, bass.IndirectOffsetOnAxis(ap=meta[par][:, j, 0:1].bitcast(U32), axis=0),
                        y_sb[par][:, j, :], None, bounds_check=TOPK * NTOK - 1,
                        oob_is_err=False).then_inc(y_scattered[par], 16)

            with pool.Fori(0, quads) as quad:
                scatter_y(quad, 0)
                scatter_y(quad, 1)

            with pool.Fori(0, NT // 2) as pair:
                for par in range(2):
                    pool.wait_ge(S["dveps_ready"], pair * 2 + par + 1)
                    pool.tensor_tensor(rstd[par][:, :], veps[par][:, :], neg_half[:, :], ALU.pow)\
                        .then_inc(S["drstd_ready"], 1)

        def quads_with_ends(eng, quads, body):
            body(0, 0, False, True)
            body(0, 1, True, True)
            with eng.Fori(1, quads - 1) as quad:
                body(quad, 0, True, True)
                body(quad, 1, True, True)
            body(quads - 1, 0, True, True)
            body(quads - 1, 1, True, False)

        @block.scalar
        def _(act):
            act.dma_start(wgu_sb[:, :], wgu).then_inc(S["big_w"], 16)
            act.dma_start(wd_sb[:, :], wd).then_inc(S["big_w"], 16)
            act.wait_ge(S["consts"], 12)
            for i in range(QUAD):
                act.dma_start(xs[NE * REGION + i * P:NE * REGION + (i + 1) * P, :], pad_rows[:, :])\
                    .then_inc(S["pads"], 16)

            def step(t):
                a, b = t.ago(1), t.ago(2)
                if b.exists:
                    act.wait_ge(S["hsT_ps"], b.n + 1)
                    act.activation(hsT_sb[:, :, :], tr_ps[:, 0:SHI], ACT.Copy).then_inc(S["hsT_copied"], 1)
                if a.exists:
                    act.wait_ge(S["oT_ps"], a.n + 1)
                    act.activation(oT_sb[:, :, :], tr_ps[:, 0:DM], ACT.Copy).then_inc(S["oT_copied"], 1)
                if t.exists:
                    act.wait_ge(S["qk_shift"], t.n + 1)
                    act.activation(att_ps[:, 0:NH * NH], shifted[:, :], ACT.Exp, scale=HD ** -0.5)\
                        .then_inc(S["p_ready"], 1)
                if t.ago(-1).exists:
                    kv_copy(t.ago(-1))
                if a.exists:
                    act.wait_ge(S["x1_ready"], a.n + 1)
                    if a.since(2):
                        act.wait_ge(scattered[a.par], a.pair * (16 * TOPK))
                    act.activation(stage[a.par][:, :, 0:DM],
                                   x1[a.par][:, :].unsqueeze(1).broadcast_to([P, TOPK, DM]),
                                   ACT.Copy).then_inc(S["staged"], 1)
                    act.wait_ge(S["x1T_ps"], a.n + 1)
                    act.activation(x1T_sb[:, :, :], tr_ps[:, 0:DM], ACT.Copy).then_inc(S["x1T_copied"], 1)
                    act.wait_ge(S["logits_ready"], a.n + 1)
                    if a.since(1):
                        act.wait_ge(S["route"], a.n * ROUTE)
                    act.activation(eneg[:, :], y_ps[:, DM:DM + NE], ACT.Exp, scale=-1.0)\
                        .then_inc(S["eneg_ready"], 1)
                    act.wait_ge(S["gu_ready"], a.n + 1)
                    act.activation(th_sb[:, :], gu_ps[:, 0:SHI], ACT.Tanh, scale=0.5)\
                        .then_inc(S["th_ready"], 1)

            def kv_copy(t):
                act.wait_ge(S["qkv_ready"], t.n + 1)
                if t.since(2):
                    act.wait_ge(S["pv_prod"], t.n - 1)
                act.activation(kv_sb[t.par][:, :], kv_ps[:, :], ACT.Copy).then_inc(S["kv_copied"], 1)

            kv_copy(Tile(0, 0))
            each_step(act, 0, NT + 1, 1, 2, step)

            act.wait_ge(S["tab_ready"], 1)
            with act.Fori(0, NE) as e:
                row = act.value_load(tab[0:1, bass.ds(e + 2 * SLOTS, 1)], min_val=0, max_val=XROWS - P)
                act.dma_start(xs[bass.ds(row, P), :], pad_rows[:, :]).then_inc(S["filled"], 16)

            quads = n_quads(act)

            def copy_xT(n):
                act.wait_ge(S["cX_ps"], n + 1)
                act.activation(xtT[:, :], banks[2][:, :], ACT.Copy).then_inc(S["cX_copied"], 1)

            def copy_y(n, par, old):
                act.wait_ge(S["cy_ps"], n + 1)
                if old is not None:
                    act.wait_ge(y_scattered[par], old)
                act.activation(y_sb[par][:, :, :], banks[6 + par][:, :], ACT.Copy)\
                    .then_inc(S["cy_copied"], 1)

            def pairs(quad, par, has_prev, has_next):
                n = quad * 2 + par
                if has_next:
                    copy_xT(n + 1)
                act.wait_ge(S["cgu_ps"], n + 1)
                act.activation(cth[par][:, :, :],
                               banks[par][:, :].rearrange("p (j f) -> p j f", j=2)[:, :, 0:EI],
                               ACT.Tanh, scale=0.5).then_inc(S["cth_ready"], 1)
                if has_prev:
                    first = isinstance(n, int) and n < 3
                    copy_y(n - 1, 1 - par, None if first else (quad * 32 if par else quad * 32 - 32))

            copy_xT(0)
            quads_with_ends(act, quads, pairs)
            copy_y(quads * 2 - 1, 1, quads * 32 - 32)

            with act.Fori(0, NT // 2) as pair:
                for par in range(2):
                    act.wait_ge(S["o2_ready"], pair * 2 + par + 1)
                    act.dma_start(out[bass.ds((pair * 2 + par) * P, P), :], o2[par][:, :])\
                        .then_inc(stored[par], 16)
            act.wait_ge(stored[0], 16 * (NT // 2))
            act.wait_ge(stored[1], 16 * (NT // 2))

        @block.tensor
        def _(pe):
            pe.wait_ge(S["consts"], 12)
            pe.wait_ge(S["small_w"], NSMALL)

            def mm(dst, lhsT, rhs, k, n):
                return pe.matmul(dst, lhsT, rhs, start=(k == 0), stop=(k == n - 1))

            def qkv(t):
                pe.wait_ge(x_loaded[t.par], t.pair * 32 + 32)
                if t.since(2):
                    pe.wait_ge(S["qk_prod"], t.n - 1)
                for k in range(KC):
                    mm(q_ps[t.par][:, 0:DM], xT_sb[t.par][:, k, :], wqkv_sb[:, k, 0:DM], k, KC)
                if t.since(1):
                    pe.wait_ge(S["kv_copied"], t.n)
                for k in range(KC):
                    last = mm(kv_ps[:, :], xT_sb[t.par][:, k, :], wqkv_sb[:, k, DM:3 * DM], k, KC)
                last.then_inc(S["qkv_ready"], 1)

            def shared_down(b):
                pe.wait_ge(S["hs_ready"], b.n + 1)
                for k in range(SHI // P):
                    last = pe.transpose(tr_ps[:, k * P:(k + 1) * P], hs_sb[:, k * P:(k + 1) * P], ident[:, :])
                last.then_inc(S["hsT_ps"], 1)
                pe.wait_ge(S["hsT_copied"], b.n + 1)
                if b.since(1):
                    pe.wait_ge(S["rk"], b.n * RK)
                for k in range(SHI // P):
                    last = mm(misc_ps[:, 0:DM], hsT_sb[:, k, :], wsd_sb[:, k, :], k, SHI // P)
                last.then_inc(S["sd_ready"], 1)

            def project(a):
                pe.wait_ge(S["att_ready"], a.n + 1)
                for k in range(KC):
                    last = pe.transpose(tr_ps[:, k * P:(k + 1) * P], o_sb[:, k * P:(k + 1) * P], ident[:, :])
                last.then_inc(S["oT_ps"], 1)
                pe.wait_ge(S["oT_copied"], a.n + 1)
                if a.since(1):
                    pe.wait_ge(S["eneg_ready"], a.n)
                for k in range(KC):
                    last = mm(y_ps[:, 0:DM], oT_sb[:, k, :], wfc_sb[:, k, :], k, KC)
                last.then_inc(S["y_ready"], 1)

            def logits_and_shared_up(a):
                pe.wait_ge(S["x1_ready"], a.n + 1)
                for k in range(KC):
                    last = pe.transpose(tr_ps[:, k * P:(k + 1) * P], x1[a.par][:, k * P:(k + 1) * P], ident[:, :])
                last.then_inc(S["x1T_ps"], 1)
                pe.wait_ge(S["x1T_copied"], a.n + 1)
                for k in range(KC):
                    last = mm(y_ps[:, DM:DM + NE], x1T_sb[:, k, :], wr_sb[:, k, :], k, KC)
                last.then_inc(S["logits_ready"], 1)
                if a.since(1):
                    pe.wait_ge(S["hs_ready"], a.n)
                for k in range(KC):
                    last = mm(gu_ps[:, :], x1T_sb[:, k, :], wsgu_sb[:, k, :], k, KC)
                last.then_inc(S["gu_ready"], 1)

            def ranks(b):
                pe.wait_ge(S["picks_ready"], 2 * b.n + 3)
                pe.wait_ge(S["sx_ready"], b.n + 1)
                mm(misc_ps[:, DM:DM + NE], before_b[:, :], picks[b.par][:, :], 0, 2)
                mm(misc_ps[:, DM:DM + NE], ones_b[:, :], seen[b.par][:, :], 1, 2)\
                    .then_inc(S["rank_ready"], 1)

            def step(t):
                a, b = t.ago(1), t.ago(2)
                if b.exists:
                    shared_down(b)
                if a.exists:
                    project(a)
                if t.ago(-1).exists:
                    qkv(t.ago(-1))
                if a.exists:
                    logits_and_shared_up(a)
                if b.exists:
                    ranks(b)

            qkv(Tile(0, 0))
            each_step(pe, 0, NT + 1, 1, 2, step)

            pe.wait_ge(S["rk"], NT * RK)
            mm(misc_ps[:, 0:NE], ones_b[:, :], seen[NT % 2][:, :], 0, 1).then_inc(S["count_ready"], 1)
            pe.wait_ge(S["b"], BSTEPS)
            for c in range(4):
                last = pe.transpose(tr_ps[0:1, c * P:(c + 1) * P], slot_row[:, c:c + 1], ident[:, :])
            last.then_inc(S["tabT"], 1)

            pe.wait_ge(S["big_w"], 32)
            quads = n_quads(pe)

            def transposes(n, par, quad):
                pe.wait_ge(xt_loaded[par], quad * 32 + 32)
                if not (isinstance(n, int) and n < 1):
                    pe.wait_ge(S["cX_copied"], n)
                for j in range(2):
                    for k in range(KC):
                        c = (j * KC + k) * P
                        last = pe.transpose(banks[2][:, c:c + P], xt[par][:, j, k * P:(k + 1) * P], ident[:, :])
                last.then_inc(S["cX_ps"], 1)

            def weight_offset(quad, par, j):
                return pe.value_load(tab[0:1, bass.ds(quad * QUAD + (SLOTS + 2 * par + j), 1)],
                                     min_val=0, max_val=(NE - 1) * KC * 2 * EI)

            def pairs(quad, par, has_prev, has_next):
                n = quad * 2 + par
                woffs = [weight_offset(quad, par, j) for j in range(2)]
                for j in range(2):
                    woff = woffs[j]
                    if j == 0:
                        pe.wait_ge(S["cX_copied"], n + 1)
                        if not (isinstance(n, int) and n < 2):
                            pe.wait_ge(S["ch_ready"], 2 * n - 2)
                    for k in range(KC):
                        c = (j * KC + k) * P
                        last = mm(banks[par][:, j * 2 * EI:(j + 1) * 2 * EI], xtT[:, c:c + P],
                                  wgu_sb[:, bass.ds(woff + k * 2 * EI, 2 * EI)], k, KC)
                    if j == 0 and has_prev:
                        transpose_h(n - 1)
                last.then_inc(S["cgu_ps"], 1)
                if has_prev:
                    down(n - 1, 1 - par, quad if par else quad - 1)
                if has_next:
                    transposes(n + 1, 1 - par, quad if par == 0 else quad + 1)

            def transpose_h(n):
                pe.wait_ge(S["ch_ready"], 2 * n + 2)
                if not (isinstance(n, int) and n < 1):
                    pe.wait_ge(S["chT_copied"], n)
                for j in range(2):
                    last = pe.transpose(banks[3][:, j * P:(j + 1) * P], ch[:, j, :], ident[:, :])
                last.then_inc(S["chT_ps"], 1)

            def down(n, par, quad):
                woffs = [weight_offset(quad, par, j) for j in range(2)]
                pe.wait_ge(S["chT_copied"], n + 1)
                if not (isinstance(n, int) and n < 2):
                    pe.wait_ge(S["cy_copied"], n - 1)
                for j in range(2):
                    last = mm(banks[6 + par][:, j * DM:(j + 1) * DM], chT[:, j * P:(j + 1) * P],
                              wd_sb[:, bass.ds(woffs[j] // 2, DM)], 0, 1)
                last.then_inc(S["cy_ps"], 1)

            transposes(0, 0, 0)
            quads_with_ends(pe, quads, pairs)
            transpose_h(quads * 2 - 1)
            down(quads * 2 - 1, 1, quads - 1)

        @block.vector
        def _(dve):
            dve.memset(gscore[:, :], -3.0e38).then_inc(S["cast"], 1)
            dve.memset(seen[0][:, :], 0.0).then_inc(S["picks_ready"], 1)
            dve.memset(ones_e[:, :], 1.0).then_inc(S["cast"], 1)
            dve.wait_ge(S["consts"], 12)
            dve.wait_ge(S["small_w"], NSMALL)
            dve.wait_ge(S["cast"], 2)
            heads = "p (h g d) -> p h g d"
            prod_v = prod[:, :].rearrange(heads, h=NH, g=NH)

            def qk(t):
                dve.wait_ge(S["qkv_ready"], t.n + 1)
                dve.wait_ge(S["kv_copied"], t.n + 1)
                dve.tensor_tensor(
                    prod_v,
                    q_ps[t.par][:, 0:DM].rearrange("p (h o d) -> p h o d", h=NH, o=1).broadcast_to([P, NH, NH, HD]),
                    kv_sb[t.par][:, 0:DM].rearrange("p (o g d) -> p o g d", o=1, g=NH).broadcast_to([P, NH, NH, HD]),
                    ALU.mult).then_inc(S["qk_prod"], 1)
                dve.wait_ge(S["qk_prod"], t.n + 1)
                dve.tensor_reduce(scores[:, :], prod[:, :].rearrange("p (s d) -> p s d", d=HD), AX, ALU.add)\
                    .then_inc(S["qk_sum"], 1)
                dve.wait_ge(S["qk_sum"], t.n + 1)
                sc = scores[:, :].rearrange("p (h g) -> p h g", h=NH)
                dve.tensor_reduce(smax[:, :], sc, AX, ALU.max).then_inc(S["qk_max"], 1)
                dve.wait_ge(S["qk_max"], t.n + 1)
                dve.tensor_tensor(shifted[:, :].rearrange("p (h g) -> p h g", h=NH), sc,
                                  smax[:, :].unsqueeze(2).broadcast_to([P, NH, NH]), ALU.subtract)\
                    .then_inc(S["qk_shift"], 1)

            def pv(t):
                dve.wait_ge(S["p_ready"], t.n + 1)
                pr = att_ps[:, 0:NH * NH].rearrange("p (h g) -> p h g", h=NH)
                dve.tensor_reduce(psum_row[:, :], pr, AX, ALU.add).then_inc(S["p_sum"], 1)
                dve.tensor_tensor(
                    prod_v,
                    att_ps[:, 0:NH * NH].rearrange("p (h o g) -> p h o g", h=NH, o=1).broadcast_to([P, NH, HD, NH]),
                    kv_sb[t.par][:, DM:2 * DM].rearrange("p (o d g) -> p o d g", o=1, g=NH).broadcast_to([P, NH, HD, NH]),
                    ALU.mult).then_inc(S["pv_prod"], 1)
                dve.wait_ge(S["p_sum"], t.n + 1)
                dve.reciprocal(prec[:, :], psum_row[:, :]).then_inc(S["p_rec"], 1)
                dve.wait_ge(S["pv_prod"], t.n + 1)
                dve.tensor_reduce(att[:, :], prod[:, :].rearrange("p (s g) -> p s g", g=NH), AX, ALU.add)\
                    .then_inc(S["pv_sum"], 1)
                dve.wait_ge(S["pv_sum"], t.n + 1)
                dve.wait_ge(S["p_rec"], t.n + 1)
                if t.since(1):
                    dve.wait_ge(S["oT_ps"], t.n)
                dve.tensor_tensor(o_sb[:, :].rearrange("p (h d) -> p h d", h=NH),
                                  att[:, :].rearrange("p (h d) -> p h d", h=NH),
                                  prec[:, :].unsqueeze(2).broadcast_to([P, NH, HD]), ALU.mult)\
                    .then_inc(S["att_ready"], 1)

            def ln1_stats(a):
                dve.wait_ge(S["y_ready"], a.n + 1)
                dve.wait_ge(x_loaded[a.par], a.pair * 32 + 32)
                dve.tensor_tensor(res[:, :], x_sb[a.par][:, :], y_ps[:, 0:DM], ALU.add)\
                    .then_inc(S["res_ready"], 1)
                dve.wait_ge(S["res_ready"], a.n + 1)
                dve.bn_stats(stats[:, :], res[:, :]).then_inc(S["st_ready"], 1)
                wait_apart(dve, S["st_ready"], a.n + 1)
                dve.bn_aggr(mv[a.par][:, :], stats[:, :]).then_inc(S["mv_ready"], 1)
                dve.wait_ge(S["mv_ready"], a.n + 1)
                dve.tensor_scalar(veps[a.par][:, :], mv[a.par][:, 1:2], EPS, None, ALU.add)\
                    .then_inc(S["veps_ready"], 1)

            def ln1_apply(a):
                dve.wait_ge(S["rstd_ready"], a.n + 1)
                if a.since(2):
                    dve.wait_ge(S["staged"], a.n - 1)
                dve.tensor_scalar(x1[a.par][:, :], res[:, :], mv[a.par][:, 0:1], rstd[a.par][:, 0:1],
                                  ALU.subtract, ALU.mult).then_inc(S["x1_ready"], 1)

            def shared_act(a):
                dve.wait_ge(S["th_ready"], a.n + 1)
                dve.scalar_tensor_tensor(out=gth_sb[:, :], in0=th_sb[:, :], scalar=1.0, in1=gu_ps[:, 0:SHI],
                                         op0=ALU.add, op1=ALU.mult).then_inc(S["gth_ready"], 1)
                dve.wait_ge(S["gth_ready"], a.n + 1)
                if a.since(1):
                    dve.wait_ge(S["hsT_ps"], a.n)
                dve.scalar_tensor_tensor(out=hs_sb[:, :], in0=gth_sb[:, :], scalar=0.5, in1=gu_ps[:, SHI:2 * SHI],
                                         op0=ALU.mult, op1=ALU.mult).then_inc(S["hs_ready"], 1)

            def shared_add(b):
                dve.wait_ge(S["sd_ready"], b.n + 1)
                dve.tensor_tensor(sx[:, bass.ds(b.n * DM, DM)], x1[b.par][:, :], misc_ps[:, 0:DM], ALU.add)\
                    .then_inc(S["sx_ready"], 1)

            def route(b):
                done = [0]

                def at(ins):
                    done[0] += 1
                    return ins.then_inc(S["route"], 1)

                def after(apart=False):
                    if apart:
                        wait_apart(dve, S["route"], b.n * ROUTE + done[0])
                    else:
                        dve.wait_ge(S["route"], b.n * ROUTE + done[0])

                dve.wait_ge(S["eneg_ready"], b.n + 1)
                at(dve.tensor_scalar(eneg1[:, :], eneg[:, :], 1.0, None, ALU.add))
                after()
                at(dve.reciprocal(sig[:, :], eneg1[:, :]))
                after()
                at(dve.tensor_tensor(sfc[:, :], sig[:, :], bias_sb[:, :], ALU.add))
                after(apart=True)
                for g in range(NGROUP):
                    at(dve.max(gtop[:, g, :], sfc[:, g * GSZ:(g + 1) * GSZ]))
                after()
                at(dve.tensor_tensor(gscore[:, 0:NGROUP], gtop[:, :, 0], gtop[:, :, 1], ALU.add))
                after(apart=True)
                at(dve.max(gbest[:, :], gscore[:, :]))
                after(apart=True)
                at(dve.max_index(gidx[:, :], gbest[:, :], gscore[:, :]))
                after()
                at(dve.tensor_copy(gidxf[:, :], gidx[:, :]))
                after()
                at(dve.tensor_scalar(gmask0[:, :], iota_e[:, 0:NGROUP], gidxf[:, 0:1], None, ALU.is_equal))
                after()
                at(dve.scalar_tensor_tensor(out=gmask[:, :], in0=iota_e[:, 0:NGROUP], scalar=gidxf[:, 1:2],
                                            in1=gmask0[:, :], op0=ALU.is_equal, op1=ALU.add))
                after()
                at(dve.tensor_tensor(masked[:, :].rearrange("p (g e) -> p g e", g=NGROUP),
                                     sfc[:, :].rearrange("p (g e) -> p g e", g=NGROUP),
                                     gmask[:, :].unsqueeze(2).broadcast_to([P, NGROUP, GSZ]), ALU.mult))
                after(apart=True)
                at(dve.max(best[:, :], masked[:, :]))
                after(apart=True)
                at(dve.max_index(bidx[:, :], best[:, :], masked[:, :]))
                after()
                at(dve.tensor_copy(bidxf[:, :], bidx[:, :]))
                after()
                at(dve.tensor_tensor(onehot[:, :, :],
                                     iota_e[:, :].unsqueeze(1).broadcast_to([P, TOPK, NE]),
                                     bidxf[:, 0:TOPK].unsqueeze(2).broadcast_to([P, TOPK, NE]), ALU.is_equal))
                after()
                if b.since(2):
                    dve.wait_ge(S["rank_ready"], b.n - 1)
                with nc.allow_low_precision(reason="zeros and ones"):
                    dve.tensor_reduce(picks[b.par][:, :], onehot[:, :, :].rearrange("p k e -> p e k"), AX,
                                      ALU.add).then_inc(S["picks_ready"], 1)
                at(dve.tensor_tensor(wsel[:, :, :], onehot[:, :, :],
                                     sig[:, :].unsqueeze(1).broadcast_to([P, TOPK, NE]), ALU.mult))
                dve.wait_ge(S["picks_ready"], 2 * b.n + 2)
                if b.since(1):
                    dve.wait_ge(S["rank_ready"], b.n)
                dve.tensor_tensor(seen[1 - b.par][:, :], seen[b.par][:, :], picks[b.par][:, :], ALU.add)\
                    .then_inc(S["picks_ready"], 1)
                after()
                at(dve.tensor_reduce(w4[:, :], wsel[:, :, :], AX, ALU.add))
                after()
                at(dve.tensor_reduce(wsum[:, :], w4[:, :], AX, ALU.add))
                after()
                at(dve.tensor_scalar(wsum1[:, :], wsum[:, :], 1e-20, None, ALU.add))
                after()
                at(dve.reciprocal(wrec[:, :], wsum1[:, :]))
                after()
                if b.since(2):
                    dve.wait_ge(scattered[b.par], b.pair * (16 * TOPK))
                at(dve.tensor_scalar(stage[b.par][:, :, WT], w4[:, :], wrec[:, 0:1], SCALE / 2,
                                     ALU.mult, ALU.mult))
                at(dve.tensor_copy(stage[b.par][:, :, ID].bitcast(U32), outid[:, :]))
                for _ in range(1):
                    at(dve.memset(stage[b.par][:, :, WT + 1:ROW], 0.0))
                after()
                at(dve.tensor_scalar(outid[:, :], outid[:, :], float(P), None, ALU.add))
                assert done[0] == ROUTE

            def positions(b):
                dve.wait_ge(S["rank_ready"], b.n + 1)
                dve.tensor_tensor(rsel[:, :, :], onehot[:, :, :],
                                  misc_ps[:, DM:DM + NE].unsqueeze(1).broadcast_to([P, TOPK, NE]),
                                  ALU.mult).then_inc(S["rk"], 1)
                dve.wait_ge(S["rk"], b.n * RK + 1)
                dve.tensor_reduce(rank[:, :], rsel[:, :, :], AX, ALU.add).then_inc(S["rk"], 1)
                dve.wait_ge(S["rk"], b.n * RK + 2)
                if b.since(2):
                    dve.wait_ge(scattered[b.par], b.pair * (16 * TOPK))
                dve.wait_ge(S["route"], (b.n + 1) * ROUTE)
                dve.scalar_tensor_tensor(out=pos[b.par][:, :], in0=bidxf[:, 0:TOPK], scalar=float(REGION),
                                         in1=rank[:, :], op0=ALU.mult, op1=ALU.add)\
                    .then_inc(S["pos_ready"], 1)

            def step(t):
                a, b = t.ago(1), t.ago(2)
                if t.exists:
                    qk(t)
                if b.exists:
                    shared_add(b)
                if a.exists:
                    ln1_stats(a)
                if b.exists:
                    route(b)
                if a.exists:
                    ln1_apply(a)
                if b.exists:
                    positions(b)
                if t.exists:
                    pv(t)
                if a.exists:
                    shared_act(a)

            each_step(dve, 0, NT + 1, 1, 2, step)

            steps = [0]

            def at(ins):
                steps[0] += 1
                return ins.then_inc(S["b"], 1)

            def after():
                dve.wait_ge(S["b"], steps[0])

            dve.wait_ge(S["count_ready"], 1)
            at(dve.tensor_scalar(cnt_u[:, :], misc_ps[:, 0:NE], float(P - 1), None, ALU.add))
            after()
            at(dve.tensor_scalar(ntile_u[:, :], cnt_u[:, :], 7, None, ALU.logical_shift_right))
            after()
            at(dve.tensor_copy(ntile[:, :], ntile_u[:, :]))
            after()
            at(dve.tensor_tensor_scan(tend[:, :], ones_e[:, :], ntile[:, :], 0.0, ALU.mult, ALU.add))
            after()
            for c in range(2):
                at(dve.tensor_scalar(past[:, c, :], tend[:, :], slot_col[:, c:c + 1], None, ALU.is_le))
            after()
            at(dve.tensor_reduce(slot_e[:, :], past[:, :, :], AX, ALU.add))
            at(dve.tensor_tensor(pend[:, :, :], past[:, :, :],
                                 tend[:, :].unsqueeze(1).broadcast_to([P, 2, NE]), ALU.mult))
            after()
            at(dve.tensor_reduce(slot_first[:, :], pend[:, :, :], AX, ALU.max))
            after()
            at(dve.tensor_tensor(slot_k[:, :], slot_col[:, :], slot_first[:, :], ALU.subtract))
            after()
            at(dve.tensor_scalar(slot_k[:, :], slot_k[:, :], float(P), None, ALU.mult))
            after()
            at(dve.scalar_tensor_tensor(out=slot_row[:, 0:2], in0=slot_e[:, :], scalar=float(REGION),
                                        in1=slot_k[:, :], op0=ALU.mult, op1=ALU.add))
            at(dve.tensor_scalar(slot_row[:, 2:4], slot_e[:, :], float(NE - 1), float(KC * 2 * EI),
                                 ALU.min, ALU.mult))
            assert steps[0] == BSTEPS
            dve.wait_ge(S["tabT"], 1)
            at(dve.tensor_copy(tab[0:1, 0:2 * SLOTS], tr_ps[0:1, 0:2 * SLOTS]))
            at(dve.tensor_tensor(tab[0:1, 2 * SLOTS:2 * SLOTS + NE], region0[0:1, :], misc_ps[0:1, 0:NE], ALU.add))
            at(dve.tensor_scalar(quadf[:, :], tend[:, NE - 1:NE], float(QUAD - 1 - 2 * QUAD), None, ALU.add))
            after()
            at(dve.tensor_scalar(tab[0:1, QUADS:QUADS + 1].bitcast(U32), quadf[0:1, :], 2, None,
                                 ALU.logical_shift_right))
            after()
            dve.memset(quadf[:, :], 0.0).then_inc(S["tab_ready"], 1)

            quads = n_quads(dve)

            def pairs(quad, par, first):
                n = quad * 2 + par
                dve.wait_ge(xt_loaded[par], quad * 32 + 32)
                if not first:
                    dve.wait_ge(y_scattered[par], quad * 32)
                dve.tensor_copy(meta[par][:, :, :], xt[par][:, :, ID:ID + 2]).then_inc(S["cmeta"], 1)
                g_u = banks[par][:, :].rearrange("p (j f) -> p j f", j=2)
                dve.wait_ge(S["cth_ready"], n + 1)
                dve.scalar_tensor_tensor(out=cgth[:, :, :], in0=cth[par][:, :, :], scalar=1.0,
                                         in1=g_u[:, :, 0:EI], op0=ALU.add, op1=ALU.mult)\
                    .then_inc(S["cgth_ready"], 1)
                dve.wait_ge(S["cgth_ready"], n + 1)
                dve.wait_ge(S["cmeta"], n + 1)
                if not (first and par == 0):
                    dve.wait_ge(S["chT_ps"], n)
                for j in range(2):
                    dve.scalar_tensor_tensor(out=ch[:, j, :], in0=cgth[:, j, :], scalar=meta[par][:, j, 1:2],
                                             in1=g_u[:, j, EI:2 * EI], op0=ALU.mult, op1=ALU.mult)\
                        .then_inc(S["ch_ready"], 1)
                dve.wait_ge(S["chT_ps"], n + 1)
                if not (first and par == 0):
                    dve.wait_ge(S["cy_ps"], n)
                dve.tensor_copy(chT[:, :], banks[3][:, 0:2 * P]).then_inc(S["chT_copied"], 1)

            pairs(0, 0, True)
            pairs(0, 1, True)
            with dve.Fori(1, quads) as quad:
                pairs(quad, 0, False)
                pairs(quad, 1, False)

            def dstep(t):
                a = t.ago(1)
                if t.exists:
                    dve.wait_ge(z_loaded[t.par], t.pair * 16 + 16)
                    dve.tensor_tensor(z2[:, :, :], zt[t.par][:, 0:2, :], zt[t.par][:, 2:4, :], ALU.add)\
                        .then_inc(S["d_a"], 1)
                    dve.wait_ge(S["d_a"], t.n + 1)
                    dve.tensor_tensor(z1[:, :], z2[:, 0, :], z2[:, 1, :], ALU.add).then_inc(S["d_b"], 1)
                    dve.wait_ge(S["d_b"], t.n + 1)
                    dve.tensor_tensor(zr[t.par][:, :], z1[:, :], sx[:, bass.ds(t.n * DM, DM)], ALU.add)\
                        .then_inc(S["zr_ready"], 1)
                    dve.wait_ge(S["zr_ready"], t.n + 1)
                    dve.bn_stats(stats[:, :], zr[t.par][:, :]).then_inc(S["dst_ready"], 1)
                    wait_apart(dve, S["dst_ready"], t.n + 1)
                    dve.bn_aggr(mv[t.par][:, :], stats[:, :]).then_inc(S["dmv_ready"], 1)
                    dve.wait_ge(S["dmv_ready"], t.n + 1)
                    dve.tensor_scalar(veps[t.par][:, :], mv[t.par][:, 1:2], EPS, None, ALU.add)\
                        .then_inc(S["dveps_ready"], 1)
                if a.exists:
                    dve.wait_ge(S["drstd_ready"], a.n + 1)
                    if a.since(2):
                        dve.wait_ge(stored[a.par], a.pair * 16)
                    dve.tensor_scalar(o2[a.par][:, :], zr[a.par][:, :], mv[a.par][:, 0:1],
                                      rstd[a.par][:, 0:1], ALU.subtract, ALU.mult)\
                        .then_inc(S["o2_ready"], 1)

            each_step(dve, 0, NT, 0, 1, dstep)


ROUTE = 27
RK = 2
BSTEPS = 13


def kernel(L0_attn_x, L0_attn_Wq, L0_attn_Wk, L0_attn_Wv, L0_attn_Wfc, L0_ffn_router_weight,
           L0_ffn_router_bias, L0_ffn_gate_w, L0_ffn_up_w, L0_ffn_down_w, L0_ffn_shared_gate_w,
           L0_ffn_shared_up_w, L0_ffn_shared_down_w):
    import numpy as np
    import concourse.bacc as bacc
    from concourse.bass_utils import run_bass_kernel_spmd

    def arr(a):
        return np.asarray(a)

    def chunked(w):
        w = arr(w)
        return np.ascontiguousarray(w.reshape(w.shape[0], -1, P).transpose(2, 1, 0))

    x = arr(L0_attn_x).reshape(NTOK, DM)
    wv = arr(L0_attn_Wv).reshape(NH, HD, DM).transpose(1, 0, 2).reshape(DM, DM)
    gate = arr(L0_ffn_gate_w).reshape(NE, EI, KC, P)
    up = arr(L0_ffn_up_w).reshape(NE, EI, KC, P)
    ins = {
        "xT": x.reshape(NT, P, KC, P).transpose(0, 3, 2, 1).reshape(NTOK, DM),
        "x": x,
        "wqkv": chunked(np.concatenate([arr(L0_attn_Wq), arr(L0_attn_Wk), wv], axis=0)),
        "wfc": chunked(L0_attn_Wfc),
        "wr": chunked(L0_ffn_router_weight),
        "rbias": np.broadcast_to(arr(L0_ffn_router_bias)[None, :], (P, NE)),
        "wsgu": chunked(np.concatenate([arr(L0_ffn_shared_gate_w), arr(L0_ffn_shared_up_w)], axis=0)),
        "wsd": chunked(L0_ffn_shared_down_w),
        "wgu": np.concatenate([gate, up], axis=1).transpose(3, 0, 2, 1).reshape(P, -1),
        "wd": arr(L0_ffn_down_w).transpose(2, 0, 1).reshape(P, -1),
    }
    nc = bacc.Bacc("TRN2", target_bir_lowering=False, num_devices=1)
    arrays, args = {}, []
    for name, a in ins.items():
        a = np.ascontiguousarray(a)
        arrays[f"in_{name}"] = a
        args.append(nc.dram_tensor(f"in_{name}", a.shape, mybir.dt.from_np(a.dtype), kind="ExternalInput").ap())
    args.append(nc.dram_tensor("out_0", (NTOK, DM), F32, kind="ExternalOutput").ap())
    build(nc, *args)
    r = run_bass_kernel_spmd(nc, [arrays], core_ids=[0])
    return r.results[0]["out_0"].reshape(4, NTOK // 4, DM)
```

```python
from contextlib import ExitStack

import concourse.bass as bass
from concourse import mybir

F32 = mybir.dt.float32
BF16 = mybir.dt.bfloat16
U32 = mybir.dt.uint32
I32 = mybir.dt.int32
ALU = mybir.AluOpType
ACT = mybir.ActivationFunctionType
AX = mybir.AxisListType.X

P = 128
NTOK, DM = 4096, 256
NT = NTOK // P
KC = DM // P
NH = 16
HD = DM // NH
NE, EI = 32, 128
TOPK, NGROUP = 4, 4
GSZ = NE // NGROUP
SHI = 256
SCALE = 2.5
NPH = 8
NDH = NH - NPH
HW = NH * HD
PD = NDH * NH
PP = NPH * NH
EPS = 1e-5
ROW = DM + 8
ID, WT = DM, DM + 1
FILL_ACT, FILL_SP = 12, 24
QUAD = 4
MAXTILES = NTOK * TOPK // P + NE - 1
SLOTS = 2 * P
REGION = NTOK + P
XROWS = NE * REGION + QUAD * P
NOWHERE = 1 << 18
assert MAXTILES + QUAD <= SLOTS


class Tile:

    def __init__(self, pair, par):
        self.pair, self.par, self.n = pair, par, pair * 2 + par

    def ago(self, k):
        q = self.par - k
        return Tile(self.pair + q // 2, q % 2)

    @property
    def exists(self):
        return not isinstance(self.n, int) or 0 <= self.n < NT

    def since(self, k):
        return not isinstance(self.n, int) or self.n >= k


def each_step(eng, first, last, lead, lag, body):
    lo = lag + lag % 2 + 2
    hi = (NT - lead) // 2 * 2
    for s in range(first, lo):
        body(Tile(s // 2, s % 2))
    with eng.Fori(lo // 2, hi // 2) as pair:
        body(Tile(pair, 0))
        body(Tile(pair, 1))
    for s in range(hi, last + 1):
        body(Tile(s // 2, s % 2))


def build(nc, xT, x, wqkv, wfc, wr, rbias, wsgu, wsd, wgu, wd, out):
    xs = nc.dram_tensor("expert_rows", [XROWS, ROW], F32).ap()
    z = nc.dram_tensor("pick_rows", [TOPK * NTOK, DM], F32).ap()

    with ExitStack() as ctx:
        def sb(name, shape, dt=F32):
            return ctx.enter_context(nc.sbuf_tensor(name, shape, dt))

        def bank(name):
            return ctx.enter_context(nc.psum_tensor(name, [P, 512], F32))

        def sem(name):
            return ctx.enter_context(nc.semaphore(name))

        wqkv_sb = sb("wqkv_sb", [P, KC, 3 * DM])
        wfc_sb = sb("wfc_sb", [P, KC, DM])
        wr_sb = sb("wr_sb", [P, KC, NE])
        bias_sb = sb("bias_sb", [P, NE])
        wsgu_sb = sb("wsgu_sb", [P, KC, 2 * SHI])
        wsd_sb = sb("wsd_sb", [P, SHI // P, DM])
        wgu_sb = sb("wgu_sb", [P, NE * KC * 2 * EI])
        wd_sb = sb("wd_sb", [P, NE * DM])
        ident = sb("ident", [P, P])
        ones_b = sb("ones_b", [P, P], BF16)
        before_b = sb("before_b", [P, P], BF16)
        iota_e = sb("iota_e", [P, NE])
        slot_col = sb("slot_col", [P, 2])
        neg_half = sb("neg_half", [P, 1])
        pad_rows = sb("pad_rows", [P, ROW])
        xT_sb = [sb(f"xT_sb{i}", [P, KC, P]) for i in range(2)]
        x_sb = [sb(f"x_sb{i}", [P, DM]) for i in range(2)]
        k_sb = [sb(f"k_sb{i}", [P, DM]) for i in range(2)]
        v_sb = [sb(f"v_sb{i}", [P, DM]) for i in range(2)]
        q_sb = [sb(f"q_sb{i}", [P, NPH * HD]) for i in range(2)]
        prod = sb("prod", [P, (NDH + 2 * NPH) * HW])
        prod_d = prod[:, 0:NDH * HW]
        prod_q = prod[:, NDH * HW:NH * HW]
        prod_p = prod[:, NH * HW:(NH + NPH) * HW]
        scores = sb("scores", [P, PD])
        smax = sb("smax", [P, NH])
        shifted = sb("shifted", [P, NH * NH])
        psum_row = sb("psum_row", [P, NH])
        prec = sb("prec", [P, NH])
        p_sb = sb("p_sb", [P, PP])
        att = sb("att", [P, NDH * HD])
        o_sb = sb("o_sb", [P, DM])
        ohT_sb = sb("ohT_sb", [P, KC + SHI // P, P])
        res = sb("res", [P, DM])
        stats = sb("stats", [P, 6])
        mv = [sb(f"mv{i}", [P, 2]) for i in range(2)]
        veps = [sb(f"veps{i}", [P, 1]) for i in range(2)]
        rstd = [sb(f"rstd{i}", [P, 1]) for i in range(2)]
        x1 = [sb(f"x1_{i}", [P, DM]) for i in range(2)]
        x1T_sb = sb("x1T_sb", [P, KC, P])
        th_sb = sb("th_sb", [P, SHI])
        gth_sb = sb("gth_sb", [P, SHI])
        hs_sb = sb("hs_sb", [P, SHI])
        sx = sb("sx", [P, NT * DM])
        eneg = sb("eneg", [P, NE])
        eneg1 = sb("eneg1", [P, NE])
        sig = sb("sig", [P, NE])
        sfc = sb("sfc", [P, NE])
        gtop = sb("gtop", [P, NGROUP, 8])
        gscore = sb("gscore", [P, 8])
        gbest = sb("gbest", [P, 8])
        gidx = sb("gidx", [P, 8], U32)
        gidxf = sb("gidxf", [P, 8])
        gmask0 = sb("gmask0", [P, NGROUP])
        gmask = sb("gmask", [P, NGROUP])
        masked = sb("masked", [P, NE])
        best = sb("best", [P, 8])
        bidx = sb("bidx", [P, 8], U32)
        bidxf = sb("bidxf", [P, 8])
        onehot = sb("onehot", [P, TOPK, NE])
        wsel = sb("wsel", [P, TOPK, NE])
        w4 = sb("w4", [P, TOPK])
        wsum = sb("wsum", [P, 1])
        wsum1 = sb("wsum1", [P, 1])
        wrec = sb("wrec", [P, 1])
        picks = [sb(f"picks{i}", [P, NE], BF16) for i in range(2)]
        seen = [sb(f"seen{i}", [P, NE], BF16) for i in range(2)]
        rsel = sb("rsel", [P, TOPK, NE])
        rank = sb("rank", [P, TOPK])
        pos = [sb(f"pos{i}", [P, TOPK], U32) for i in range(2)]
        outid = sb("outid", [P, TOPK], U32)
        stage = [sb(f"stage{i}", [P, TOPK, ROW]) for i in range(2)]
        cnt_u = sb("cnt_u", [P, NE], U32)
        ntile_u = sb("ntile_u", [P, NE], U32)
        ntile = sb("ntile", [P, NE])
        ones_e = sb("ones_e", [P, NE])
        tend = sb("tend", [P, NE])
        past = sb("past", [P, 2, NE])
        pend = sb("pend", [P, 2, NE])
        slot_e = sb("slot_e", [P, 2])
        slot_first = sb("slot_first", [P, 2])
        slot_k = sb("slot_k", [P, 2])
        slot_row = sb("slot_row", [P, 4])
        region0 = sb("region0", [P, NE])
        tab = sb("tab", [1, 2 * SLOTS + NE + 8], I32)
        quadf = sb("quadf", [P, 1], U32)
        ids = [sb(f"ids{i}", [P, 2], U32) for i in range(2)]
        meta = [sb(f"meta{i}", [P, 2, 2]) for i in range(2)]
        def over_prod(at, *shape):
            size = 1
            for s in shape:
                size *= s
            part = prod[:, at:at + size]
            return part.rearrange("p (a b) -> p a b", a=shape[0]) if len(shape) > 1 else part

        xtT = [over_prod(i * 2 * DM, 2 * KC * P) for i in range(2)]
        chT = over_prod(4 * DM, 2 * P)
        y_sb = [over_prod((5 + 2 * i) * DM, 2, DM) for i in range(2)]
        xt = [over_prod(9 * DM + i * 2 * ROW, 2, ROW) for i in range(2)]
        cth = [over_prod(9 * DM + 4 * ROW + i * 2 * EI, 2, EI) for i in range(2)]
        cgth = over_prod(9 * DM + 4 * ROW + 4 * EI, 2, EI)
        ch = over_prod(9 * DM + 4 * ROW + 6 * EI, 2, EI)
        zt = [over_prod(i * TOPK * DM, TOPK, DM) for i in range(2)]
        z2 = [over_prod((8 + 2 * i) * DM, 2, DM) for i in range(2)]
        o2 = [over_prod((12 + i) * DM, DM) for i in range(2)]

        banks = [bank(f"bank{i}") for i in range(8)]
        qs_ps = banks[0:2]
        QKS, PVS = DM, DM + PP
        kv_ps = banks[2]
        tr_ps = banks[3]
        y_ps = banks[4]
        gu_ps = banks[5]
        att_ps = banks[6]
        misc_ps = banks[7]

        SEMS = """xT_loaded0 xT_loaded1 x_loaded0 x_loaded1 small_w big_w consts pads cast
        q_ready kv_ready q_copied k_copied v_copied qk_prod_d qk_prod_p qk_sum_d qk_sum_p qk_max qk_shift
        p_ready_d p_ready_p p_sum p_rec pv_prod_d pv_prod_p pv_sum_d pv_sum_p att_ready
        ohT_ps ohT_copied y_ready res_ready st_ready mv_ready veps_ready rstd_ready x1_ready staged
        x1T_ps x1T_copied logits_ready gu_ready eneg_ready th_ready gth_ready hs_ready
        sd_ready sx_ready route picks_ready rank_ready rk pos_ready scat0 scat1
        count_ready b tabT tab_ready filled_act filled_sp filled_pool
        xt0 xt1 cX_ps cX_copied cmeta ids_ready cgu_ps cth_ready cgth_ready ch_ready chT_ps chT_copied cy_ps cy_copied
        yscat0 yscat1
        z_loaded0 z_loaded1 d_a d_ps dst_ready dmv_ready dveps_ready drstd_ready o2_ready
        stored0 stored1""".split()
        S = {name: sem(name) for name in SEMS}
        xT_loaded = [S["xT_loaded0"], S["xT_loaded1"]]
        x_loaded = [S["x_loaded0"], S["x_loaded1"]]
        scattered = [S["scat0"], S["scat1"]]
        xt_loaded = [S["xt0"], S["xt1"]]
        y_scattered = [S["yscat0"], S["yscat1"]]
        z_loaded = [S["z_loaded0"], S["z_loaded1"]]
        stored = [S["stored0"], S["stored1"]]

        NSMALL = 6 * 16
        QUADS = 2 * SLOTS + NE

        block = ctx.enter_context(nc.Block())

        def wait_apart(eng, semaphore, value):
            goal = value if isinstance(value, int) else eng.snap(eng.to_reg(value))
            eng.wait_ge(S["consts"], 12)
            eng.wait_ge(semaphore, goal)

        def n_quads(eng):
            eng.wait_ge(S["tab_ready"], 1)
            return eng.value_load(tab[0:1, QUADS:QUADS + 1], min_val=NTOK * TOPK // P // QUAD - 2,
                                  max_val=(MAXTILES + QUAD - 1) // QUAD - 2) + 2

        def fill_padding(eng, first, last, filled):
            with eng.Fori(first, last) as e:
                row = eng.value_load(tab[0:1, bass.ds(e + 2 * SLOTS, 1)], min_val=0, max_val=XROWS - P)
                eng.dma_start(xs[bass.ds(row, P), :], pad_rows[:, :]).then_inc(filled, 16)

        @block.sync
        def _(sp):
            sp.dma_start(wqkv_sb[:, :, :], wqkv).then_inc(S["small_w"], 16)

            def load_xT(t):
                if t.since(2):
                    sp.wait_ge(S["kv_ready"], t.n - 1)
                sp.dma_start(xT_sb[t.par][:, :, :], xT[bass.ds(t.n * P, P), :]).then_inc(xT_loaded[t.par], 16)

            def load_expert(e):
                for dst, src, width in ((wgu_sb, wgu, KC * 2 * EI), (wd_sb, wd, DM)):
                    sp.dma_start(dst[:, bass.ds(e * width, width)], src[:, bass.ds(e * width, width)])\
                        .then_inc(S["big_w"], 16)

            def load_x(t):
                if t.since(2):
                    sp.wait_ge(S["res_ready"], t.n - 1)
                sp.dma_start(x_sb[t.par][:, :], x[bass.ds(t.n * P, P), :]).then_inc(x_loaded[t.par], 16)

            def step(t):
                b = t.ago(3)
                if t.exists:
                    load_xT(t)
                if b.exists:
                    load_x(b)
                    load_expert(b.n)

            step(Tile(0, 0))
            step(Tile(0, 1))
            for dst, src in ((wfc_sb[:, :, :], wfc), (wr_sb[:, :, :], wr), (wsgu_sb[:, :, :], wsgu),
                             (wsd_sb[:, :, :], wsd), (bias_sb[:, :], rbias)):
                sp.dma_start(dst, src).then_inc(S["small_w"], 16)
            each_step(sp, 2, NT + 2, 0, 3, step)

            quads = n_quads(sp)
            fill_padding(sp, FILL_ACT, FILL_SP, S["filled_sp"])
            for par in range(2):
                sp.wait_ge(scattered[par], 16 * TOPK * (NT // 2))
            sp.wait_ge(S["filled_act"], 16 * FILL_ACT)
            sp.wait_ge(S["filled_sp"], 16 * (FILL_SP - FILL_ACT))
            sp.wait_ge(S["filled_pool"], 16 * (NE - FILL_SP))
            sp.wait_ge(S["pads"], 16 * QUAD)

            def load_rows(pair, par, first):
                if not first:
                    sp.wait_ge(S["cX_ps"], 2 * pair + par - 1)
                    sp.wait_ge(S["cmeta"], 2 * pair + par - 1)
                for j in range(2):
                    row = sp.value_load(tab[0:1, bass.ds(pair * QUAD + 2 * par + j, 1)],
                                        min_val=0, max_val=XROWS - P)
                    sp.dma_start(xt[par][:, j, :], xs[bass.ds(row, P), :]).then_inc(xt_loaded[par], 16)

            load_rows(0, 0, True)
            load_rows(0, 1, True)
            with sp.Fori(1, quads) as quad:
                load_rows(quad, 0, False)
                load_rows(quad, 1, False)

            for par in range(2):
                sp.wait_ge(y_scattered[par], quads * 32)

            def load_z(t):
                if t.since(2):
                    sp.wait_ge(S["d_a"], t.n - 1)
                sp.dma_start(zt[t.par][:, :, :],
                             z.rearrange("(k n) c -> n k c", k=TOPK)[bass.ds(t.n * P, P), :, :])\
                    .then_inc(z_loaded[t.par], 16)

            load_z(Tile(0, 0))
            load_z(Tile(0, 1))
            with sp.Fori(1, NT // 2) as pair:
                load_z(Tile(pair, 0))
                load_z(Tile(pair, 1))

        @block.gpsimd
        def _(pool):
            pool.memset(ident[:, :], 1.0).then_inc(S["consts"], 1)
            pool.memset(before_b[:, :], 1.0).then_inc(S["consts"], 1)
            pool.memset(ones_b[:, :], 1.0).then_inc(S["consts"], 1)
            pool.memset(neg_half[:, :], -0.5).then_inc(S["consts"], 1)
            pool.memset(pad_rows[:, :], 0.0).then_inc(S["consts"], 1)
            pool.iota(iota_e[:, :], [[1, NE]], base=0, channel_multiplier=0,
                      allow_small_or_imprecise_dtypes=True).then_inc(S["consts"], 1)
            pool.iota(slot_col[:, :], [[P, 2]], base=0, channel_multiplier=1,
                      allow_small_or_imprecise_dtypes=True).then_inc(S["consts"], 1)
            pool.iota(region0[:, :], [[REGION, NE]], base=0, channel_multiplier=0,
                      allow_small_or_imprecise_dtypes=True).then_inc(S["consts"], 1)
            pool.iota(outid[:, :], [[NTOK, TOPK]], base=0, channel_multiplier=1).then_inc(S["consts"], 1)
            pool.wait_ge(S["consts"], 9)
            pool.affine_select(out=ident[:, :], in_=ident[:, :], compare_op=ALU.is_equal, fill=0.0,
                               base=0, pattern=[[-1, P]], channel_multiplier=1).then_inc(S["consts"], 1)
            pool.affine_select(out=before_b[:, :], in_=before_b[:, :], compare_op=ALU.is_gt, fill=0.0,
                               base=0, pattern=[[1, P]], channel_multiplier=-1).then_inc(S["consts"], 1)
            pool.iota(pad_rows[:, ID:ID + 1].bitcast(U32), [[0, 1]], base=NOWHERE,
                      channel_multiplier=0).then_inc(S["consts"], 1)

            def scatter_rows(d):
                wait_apart(pool, S["pos_ready"], d.n + 1)
                for k in range(TOPK):
                    pool.indirect_dma_start(
                        xs, bass.IndirectOffsetOnAxis(ap=pos[d.par][:, k:k + 1], axis=0),
                        stage[d.par][:, k, :], None, bounds_check=XROWS - 1,
                        oob_is_err=False).then_inc(scattered[d.par], 16)

            def step(t):
                c, a, d = t.ago(1), t.ago(2), t.ago(4)
                if t.exists:
                    if t.since(1):
                        pool.wait_ge(S["qk_sum_p"], t.n)
                    pool.wait_ge(S["q_copied"], t.n + 1)
                    pool.wait_ge(S["k_copied"], t.n + 1)
                    pool.tensor_tensor(
                        prod_q.rearrange("p (d h g) -> p d h g", d=HD, h=NPH),
                        q_sb[t.par][:, :].rearrange("p (h d o) -> p d h o", h=NPH, o=1).broadcast_to([P, HD, NPH, NH]),
                        k_sb[t.par][:, :].rearrange("p (g d o) -> p d o g", g=NH, o=1).broadcast_to([P, HD, NPH, NH]),
                        ALU.mult).then_inc(S["qk_prod_p"], 1)
                if a.exists:
                    pool.wait_ge(S["veps_ready"], a.n + 1)
                    pool.tensor_tensor(rstd[a.par][:, :], veps[a.par][:, :], neg_half[:, :], ALU.pow)\
                        .then_inc(S["rstd_ready"], 1)
                if c.exists:
                    if c.since(1):
                        pool.wait_ge(S["pv_sum_p"], c.n)
                    pool.wait_ge(S["p_ready_p"], c.n + 1)
                    pool.wait_ge(S["v_copied"], c.n + 1)
                    pool.tensor_tensor(
                        prod_p.rearrange("p (g h d) -> p g h d", g=NH, h=NPH),
                        p_sb[:, :].rearrange("p (h g o) -> p g h o", h=NPH, o=1).broadcast_to([P, NH, NPH, HD]),
                        v_sb[c.par][:, :].rearrange("p (d g o) -> p g o d", g=NH, o=1).broadcast_to([P, NH, NPH, HD]),
                        ALU.mult).then_inc(S["pv_prod_p"], 1)
                if d.exists:
                    scatter_rows(d)

            each_step(pool, 0, NT + 3, 0, 4, step)

            quads = n_quads(pool)
            fill_padding(pool, FILL_SP, NE, S["filled_pool"])

            def scatter_y(pair, par):
                wait_apart(pool, S["ids_ready"], pair * 2 + par + 1)
                wait_apart(pool, S["cy_copied"], pair * 2 + par + 1)
                for j in range(2):
                    pool.indirect_dma_start(
                        z, bass.IndirectOffsetOnAxis(ap=ids[par][:, j:j + 1], axis=0),
                        y_sb[par][:, j, :], None, bounds_check=TOPK * NTOK - 1,
                        oob_is_err=False).then_inc(y_scattered[par], 16)

            with pool.Fori(0, quads) as quad:
                scatter_y(quad, 0)
                scatter_y(quad, 1)

            with pool.Fori(0, NT // 2) as pair:
                for par in range(2):
                    pool.wait_ge(S["dveps_ready"], pair * 2 + par + 1)
                    pool.tensor_tensor(rstd[par][:, :], veps[par][:, :], neg_half[:, :], ALU.pow)\
                        .then_inc(S["drstd_ready"], 1)

        def quads_with_ends(eng, quads, body):
            body(0, 0, False, True)
            body(0, 1, True, True)
            with eng.Fori(1, quads - 1) as quad:
                body(quad, 0, True, True)
                body(quad, 1, True, True)
            body(quads - 1, 0, True, True)
            body(quads - 1, 1, True, False)

        @block.scalar
        def _(act):
            act.wait_ge(S["consts"], 12)
            for i in range(QUAD):
                act.dma_start(xs[NE * REGION + i * P:NE * REGION + (i + 1) * P, :], pad_rows[:, :])\
                    .then_inc(S["pads"], 16)

            def copy_qk(t):
                act.wait_ge(S["q_ready"], t.n + 1)
                if t.since(2):
                    act.wait_ge(S["qk_prod_p"], t.n - 1)
                act.activation(q_sb[t.par][:, :], qs_ps[t.par][:, NDH * HD:DM], ACT.Copy)\
                    .then_inc(S["q_copied"], 1)
                act.wait_ge(S["kv_ready"], t.n + 1)
                if t.since(2):
                    act.wait_ge(S["qk_prod_d"], t.n - 1)
                act.activation(k_sb[t.par][:, :], kv_ps[:, 0:DM], ACT.Copy).then_inc(S["k_copied"], 1)

            def copy_v(t):
                if t.since(2):
                    act.wait_ge(S["pv_prod_d"], t.n - 1)
                    act.wait_ge(S["pv_prod_p"], t.n - 1)
                act.wait_ge(S["kv_ready"], t.n + 1)
                act.activation(v_sb[t.par][:, :], kv_ps[:, DM:2 * DM], ACT.Copy).then_inc(S["v_copied"], 1)

            def step(t):
                c, a, b = t.ago(1), t.ago(2), t.ago(3)
                if a.exists or b.exists:
                    act.wait_ge(S["ohT_ps"], t.n - 1)
                    lo, hi = 0 if a.exists else KC, KC + SHI // P if b.exists else KC
                    act.activation(ohT_sb[:, lo:hi, :], tr_ps[:, lo * P:hi * P], ACT.Copy)\
                        .then_inc(S["ohT_copied"], 1)
                if t.ago(-1).exists:
                    copy_qk(t.ago(-1))
                if b.exists:
                    if b.since(2):
                        act.wait_ge(scattered[b.par], b.pair * (16 * TOPK))
                    act.wait_ge(S["x1_ready"], b.n + 1)
                    act.activation(stage[b.par][:, :, 0:DM],
                                   x1[b.par][:, :].unsqueeze(1).broadcast_to([P, TOPK, DM]),
                                   ACT.Copy).then_inc(S["staged"], 1)
                if a.exists:
                    act.wait_ge(S["x1T_ps"], a.n + 1)
                    act.activation(x1T_sb[:, :, :], tr_ps[:, 0:DM], ACT.Copy).then_inc(S["x1T_copied"], 1)
                    act.wait_ge(S["logits_ready"], a.n + 1)
                    if a.since(1):
                        act.wait_ge(S["route"], a.n * ROUTE - (ROUTE - 1))
                    act.activation(eneg[:, :], y_ps[:, DM:DM + NE], ACT.Exp, scale=-1.0)\
                        .then_inc(S["eneg_ready"], 1)
                if t.ago(-1).exists:
                    copy_v(t.ago(-1))
                if a.exists:
                    act.wait_ge(S["gu_ready"], a.n + 1)
                    act.activation(th_sb[:, :], gu_ps[:, 0:SHI], ACT.Tanh, scale=0.5)\
                        .then_inc(S["th_ready"], 1)
                if t.exists:
                    act.wait_ge(S["qk_shift"], 2 * t.n + 2)
                    if c.exists:
                        act.wait_ge(S["pv_prod_d"], c.n + 1)
                        act.wait_ge(S["pv_prod_p"], c.n + 1)
                        act.wait_ge(S["p_sum"], 2 * c.n + 2)
                    act.activation(att_ps[:, 0:PD], shifted[:, 0:PD], ACT.Exp, scale=HD ** -0.5)\
                        .then_inc(S["p_ready_d"], 1)
                    act.activation(p_sb[:, :], shifted[:, PD:PD + PP], ACT.Exp, scale=HD ** -0.5)\
                        .then_inc(S["p_ready_p"], 1)

            copy_qk(Tile(0, 0))
            copy_v(Tile(0, 0))
            each_step(act, 0, NT + 3, 1, 4, step)

            act.wait_ge(S["tab_ready"], 1)
            fill_padding(act, 0, FILL_ACT, S["filled_act"])

            quads = n_quads(act)

            def copy_xT(n, par):
                act.wait_ge(S["cX_ps"], n + 1)
                if not (isinstance(n, int) and n < 2):
                    act.wait_ge(S["cgu_ps"], n - 1)
                act.activation(xtT[par][:, :], banks[2][:, :], ACT.Copy).then_inc(S["cX_copied"], 1)

            def copy_y(n, par, old):
                act.wait_ge(S["cy_ps"], n + 1)
                if old is not None:
                    act.wait_ge(y_scattered[par], old)
                act.activation(y_sb[par][:, :, :], banks[6 + par][:, :], ACT.Copy)\
                    .then_inc(S["cy_copied"], 1)

            def pairs(quad, par, has_prev, has_next):
                n = quad * 2 + par
                if has_next:
                    copy_xT(n + 1, 1 - par)
                act.wait_ge(S["cgu_ps"], n + 1)
                act.activation(cth[par][:, :, :],
                               banks[par][:, :].rearrange("p (j f) -> p j f", j=2)[:, :, 0:EI],
                               ACT.Tanh, scale=0.5).then_inc(S["cth_ready"], 1)
                if has_prev:
                    first = isinstance(n, int) and n < 3
                    copy_y(n - 1, 1 - par, None if first else (quad * 32 if par else quad * 32 - 32))

            copy_xT(0, 0)
            quads_with_ends(act, quads, pairs)
            copy_y(quads * 2 - 1, 1, quads * 32 - 32)

            with act.Fori(0, NT // 2) as pair:
                for par in range(2):
                    act.wait_ge(S["o2_ready"], pair * 2 + par + 1)
                    act.dma_start(out[bass.ds((pair * 2 + par) * P, P), :], o2[par][:, :])\
                        .then_inc(stored[par], 16)
            act.wait_ge(stored[0], 16 * (NT // 2))
            act.wait_ge(stored[1], 16 * (NT // 2))

        @block.tensor
        def _(pe):
            pe.wait_ge(S["consts"], 12)
            pe.wait_ge(S["small_w"], NSMALL)

            def mm(dst, lhsT, rhs, k, n):
                return pe.matmul(dst, lhsT, rhs, start=(k == 0), stop=(k == n - 1))

            def project_q(t):
                pe.wait_ge(xT_loaded[t.par], t.pair * 16 + 16)
                if t.since(2):
                    pe.wait_ge(S["qk_shift"], 2 * t.n - 2)
                for k in range(KC):
                    last = mm(qs_ps[t.par][:, 0:DM], xT_sb[t.par][:, k, :], wqkv_sb[:, k, 0:DM], k, KC)
                last.then_inc(S["q_ready"], 1)

            def project_kv(t):
                if t.since(1):
                    pe.wait_ge(S["v_copied"], t.n)
                for k in range(KC):
                    last = mm(kv_ps[:, :], xT_sb[t.par][:, k, :], wqkv_sb[:, k, DM:3 * DM], k, KC)
                last.then_inc(S["kv_ready"], 1)

            def sum_products(dst, products):
                for i in range(HD):
                    last = mm(dst, ident[:, :], products[:, i * PP:(i + 1) * PP], i, HD)
                return last

            def step(t):
                c, a, b = t.ago(1), t.ago(2), t.ago(3)
                if a.exists or b.exists:
                    if b.exists:
                        pe.wait_ge(S["x1T_copied"], b.n + 1)
                if b.exists:
                    pe.wait_ge(S["hs_ready"], b.n + 1)
                    for k in range(SHI // P):
                        last = pe.transpose(tr_ps[:, (KC + k) * P:(KC + k + 1) * P],
                                            hs_sb[:, k * P:(k + 1) * P], ident[:, :])
                if a.exists:
                    pe.wait_ge(S["att_ready"], 2 * a.n + 2)
                    for k in range(KC):
                        last = pe.transpose(tr_ps[:, k * P:(k + 1) * P], o_sb[:, k * P:(k + 1) * P], ident[:, :])
                if a.exists or b.exists:
                    last.then_inc(S["ohT_ps"], 1)
                if t.ago(-1).exists:
                    project_q(t.ago(-1))
                if a.exists or b.exists:
                    pe.wait_ge(S["ohT_copied"], t.n - 1)
                if a.exists:
                    if a.since(1):
                        pe.wait_ge(S["eneg_ready"], a.n)
                    for k in range(KC):
                        last = mm(y_ps[:, 0:DM], ohT_sb[:, k, :], wfc_sb[:, k, :], k, KC)
                    last.then_inc(S["y_ready"], 1)
                if b.exists:
                    if b.since(1):
                        pe.wait_ge(S["rk"], b.n * RK - (RK - 1))
                    for k in range(SHI // P):
                        last = mm(misc_ps[:, 0:DM], ohT_sb[:, KC + k, :], wsd_sb[:, k, :], k, SHI // P)
                    last.then_inc(S["sd_ready"], 1)
                if t.ago(-1).exists:
                    project_kv(t.ago(-1))
                if t.exists:
                    pe.wait_ge(S["qk_prod_p"], t.n + 1)
                    pe.wait_ge(S["qk_prod_d"], t.n + 1)
                    sum_products(qs_ps[t.par][:, QKS:QKS + PP], prod_q).then_inc(S["qk_sum_p"], 1)
                if a.exists:
                    pe.wait_ge(S["x1_ready"], a.n + 1)
                    for k in range(KC):
                        last = pe.transpose(tr_ps[:, k * P:(k + 1) * P], x1[a.par][:, k * P:(k + 1) * P],
                                            ident[:, :])
                    last.then_inc(S["x1T_ps"], 1)
                if c.exists:
                    pe.wait_ge(S["pv_prod_p"], c.n + 1)
                    if t.ago(-1).exists:
                        pe.wait_ge(S["q_copied"], t.n + 2)
                    sum_products(qs_ps[c.par][:, PVS:PVS + PP], prod_p).then_inc(S["pv_sum_p"], 1)
                if a.exists:
                    pe.wait_ge(S["x1T_copied"], a.n + 1)
                    for k in range(KC):
                        last = mm(y_ps[:, DM:DM + NE], x1T_sb[:, k, :], wr_sb[:, k, :], k, KC)
                    last.then_inc(S["logits_ready"], 1)
                    if a.since(1):
                        pe.wait_ge(S["hs_ready"], a.n)
                    for k in range(KC):
                        last = mm(gu_ps[:, :], x1T_sb[:, k, :], wsgu_sb[:, k, :], k, KC)
                    last.then_inc(S["gu_ready"], 1)
                if b.exists:
                    pe.wait_ge(S["picks_ready"], 2 * b.n + 3)
                    pe.wait_ge(S["sx_ready"], b.n + 1)
                    mm(misc_ps[:, DM:DM + NE], before_b[:, :], picks[b.par][:, :], 0, 2)
                    mm(misc_ps[:, DM:DM + NE], ones_b[:, :], seen[b.par][:, :], 1, 2)\
                        .then_inc(S["rank_ready"], 1)

            project_q(Tile(0, 0))
            project_kv(Tile(0, 0))
            each_step(pe, 0, NT + 3, 1, 4, step)

            pe.wait_ge(S["rk"], NT * RK)
            mm(misc_ps[:, 0:NE], ones_b[:, :], seen[NT % 2][:, :], 0, 1).then_inc(S["count_ready"], 1)
            pe.wait_ge(S["b"], BSTEPS)
            for c in range(4):
                last = pe.transpose(tr_ps[0:1, c * P:(c + 1) * P], slot_row[:, c:c + 1], ident[:, :])
            last.then_inc(S["tabT"], 1)

            pe.wait_ge(S["big_w"], 2 * 16 * NE)
            quads = n_quads(pe)

            def transposes(n, par, quad):
                pe.wait_ge(xt_loaded[par], quad * 32 + 32)
                if not (isinstance(n, int) and n < 1):
                    pe.wait_ge(S["cX_copied"], n)
                for j in range(2):
                    for k in range(KC):
                        c = (j * KC + k) * P
                        last = pe.transpose(banks[2][:, c:c + P], xt[par][:, j, k * P:(k + 1) * P], ident[:, :])
                last.then_inc(S["cX_ps"], 1)

            def weight_offset(quad, par, j):
                return pe.value_load(tab[0:1, bass.ds(quad * QUAD + (SLOTS + 2 * par + j), 1)],
                                     min_val=0, max_val=(NE - 1) * KC * 2 * EI)

            def pairs(quad, par, has_prev, has_next):
                n = quad * 2 + par
                if has_next:
                    transposes(n + 1, 1 - par, quad if par == 0 else quad + 1)
                woffs = [weight_offset(quad, par, j) for j in range(2)]
                for j in range(2):
                    woff = woffs[j]
                    if j == 0:
                        pe.wait_ge(S["cX_copied"], n + 1)
                        if not (isinstance(n, int) and n < 2):
                            pe.wait_ge(S["ch_ready"], 2 * n - 2)
                    for k in range(KC):
                        c = (j * KC + k) * P
                        last = mm(banks[par][:, j * 2 * EI:(j + 1) * 2 * EI], xtT[par][:, c:c + P],
                                  wgu_sb[:, bass.ds(woff + k * 2 * EI, 2 * EI)], k, KC)
                    if j == 0 and has_prev:
                        transpose_h(n - 1)
                last.then_inc(S["cgu_ps"], 1)
                if has_prev:
                    down(n - 1, 1 - par, quad if par else quad - 1)

            def transpose_h(n):
                pe.wait_ge(S["ch_ready"], 2 * n + 2)
                if not (isinstance(n, int) and n < 1):
                    pe.wait_ge(S["chT_copied"], n)
                for j in range(2):
                    last = pe.transpose(banks[3][:, j * P:(j + 1) * P], ch[:, j, :], ident[:, :])
                last.then_inc(S["chT_ps"], 1)

            def down(n, par, quad):
                woffs = [weight_offset(quad, par, j) for j in range(2)]
                pe.wait_ge(S["chT_copied"], n + 1)
                if not (isinstance(n, int) and n < 2):
                    pe.wait_ge(S["cy_copied"], n - 1)
                for j in range(2):
                    last = mm(banks[6 + par][:, j * DM:(j + 1) * DM], chT[:, j * P:(j + 1) * P],
                              wd_sb[:, bass.ds(woffs[j] // 2, DM)], 0, 1)
                last.then_inc(S["cy_ps"], 1)

            transposes(0, 0, 0)
            quads_with_ends(pe, quads, pairs)
            transpose_h(quads * 2 - 1)
            down(quads * 2 - 1, 1, quads - 1)

            def sum_rows(t):
                pe.wait_ge(S["d_a"], t.n + 1)
                if t.since(2):
                    pe.wait_ge(S["o2_ready"], t.n - 1)
                for i in range(2):
                    mm(banks[t.par][:, 0:DM], ident[:, :], z2[t.par][:, i, :], i, 3)
                mm(banks[t.par][:, 0:DM], ident[:, :], sx[:, bass.ds(t.n * DM, DM)], 2, 3)\
                    .then_inc(S["d_ps"], 1)

            each_step(pe, 0, NT - 1, 0, 0, sum_rows)

        @block.vector
        def _(dve):
            dve.memset(gscore[:, :], -3.0e38).then_inc(S["cast"], 1)
            dve.memset(seen[0][:, :], 0.0).then_inc(S["picks_ready"], 1)
            dve.memset(ones_e[:, :], 1.0).then_inc(S["cast"], 1)
            dve.wait_ge(S["consts"], 12)
            dve.wait_ge(S["small_w"], NSMALL)
            dve.wait_ge(S["cast"], 2)
            def step(t):
                c, a, b, d = t.ago(1), t.ago(2), t.ago(3), t.ago(4)
                done = [0]

                def at(ins):
                    done[0] += 1
                    return ins.then_inc(S["route"], 1)

                def after(apart=False):
                    if apart:
                        wait_apart(dve, S["route"], b.n * ROUTE + done[0])
                    else:
                        dve.wait_ge(S["route"], b.n * ROUTE + done[0])

                def qk_products(h0, h1):
                    n = h1 - h0
                    ins = dve.tensor_tensor(
                        prod_d[:, h0 * HW:h1 * HW].rearrange("p (h g d) -> p h g d", h=n, g=NH),
                        qs_ps[t.par][:, h0 * HD:h1 * HD].rearrange("p (h o d) -> p h o d", h=n, o=1)
                        .broadcast_to([P, n, NH, HD]),
                        k_sb[t.par][:, :].rearrange("p (o g d) -> p o g d", o=1, g=NH)
                        .broadcast_to([P, n, NH, HD]), ALU.mult)
                    if h1 == NDH:
                        ins.then_inc(S["qk_prod_d"], 1)

                def pv_products(h0, h1):
                    n = h1 - h0
                    ins = dve.tensor_tensor(
                        prod_d[:, h0 * HW:h1 * HW].rearrange("p (h d g) -> p h d g", h=n, d=HD),
                        att_ps[:, h0 * NH:h1 * NH].rearrange("p (h o g) -> p h o g", h=n, o=1)
                        .broadcast_to([P, n, HD, NH]),
                        v_sb[c.par][:, :].rearrange("p (o d g) -> p o d g", o=1, g=NH)
                        .broadcast_to([P, n, HD, NH]), ALU.mult)
                    if h1 == NDH:
                        ins.then_inc(S["pv_prod_d"], 1)

                if t.exists:
                    dve.wait_ge(S["q_ready"], t.n + 1)
                    dve.wait_ge(S["k_copied"], t.n + 1)
                    if a.exists:
                        dve.wait_ge(S["pv_sum_p"], a.n + 1)
                    qk_products(0, NDH // 2)
                if b.exists:
                    dve.wait_ge(S["th_ready"], b.n + 1)
                    dve.scalar_tensor_tensor(out=gth_sb[:, :], in0=th_sb[:, :], scalar=1.0,
                                             in1=gu_ps[:, 0:SHI], op0=ALU.add, op1=ALU.mult)\
                        .then_inc(S["gth_ready"], 1)
                if a.exists:
                    dve.wait_ge(S["pv_sum_d"], a.n + 1)
                    dve.wait_ge(S["p_rec"], a.n + 1)
                    if a.since(1):
                        dve.wait_ge(S["ohT_ps"], a.n)
                    dve.tensor_tensor(o_sb[:, 0:NDH * HD].rearrange("p (h d) -> p h d", h=NDH),
                                      att[:, :].rearrange("p (h d) -> p h d", h=NDH),
                                      prec[:, 0:NDH].unsqueeze(2).broadcast_to([P, NDH, HD]), ALU.mult)\
                        .then_inc(S["att_ready"], 1)
                    dve.wait_ge(S["pv_sum_p"], a.n + 1)
                    dve.tensor_tensor(o_sb[:, NDH * HD:DM].rearrange("p (h d) -> p h d", h=NPH),
                                      qs_ps[a.par][:, PVS:PVS + PP].rearrange("p (h d) -> p h d", h=NPH),
                                      prec[:, NDH:NH].unsqueeze(2).broadcast_to([P, NPH, HD]), ALU.mult)\
                        .then_inc(S["att_ready"], 1)
                if b.exists:
                    dve.wait_ge(S["gth_ready"], b.n + 1)
                    if b.since(1):
                        dve.wait_ge(S["ohT_ps"], t.n - 2)
                    dve.scalar_tensor_tensor(out=hs_sb[:, :], in0=gth_sb[:, :], scalar=0.5,
                                             in1=gu_ps[:, SHI:2 * SHI], op0=ALU.mult, op1=ALU.mult)\
                        .then_inc(S["hs_ready"], 1)
                if d.exists:
                    dve.wait_ge(S["rank_ready"], d.n + 1)
                    dve.tensor_tensor(rsel[:, :, :], onehot[:, :, :],
                                      misc_ps[:, DM:DM + NE].unsqueeze(1).broadcast_to([P, TOPK, NE]),
                                      ALU.mult).then_inc(S["rk"], 1)
                if b.exists:
                    dve.wait_ge(S["eneg_ready"], b.n + 1)
                    at(dve.tensor_scalar(eneg1[:, :], eneg[:, :], 1.0, None, ALU.add))
                if d.exists:
                    dve.wait_ge(S["rk"], d.n * RK + 1)
                    dve.tensor_reduce(rank[:, :], rsel[:, :, :], AX, ALU.add).then_inc(S["rk"], 1)
                if b.exists:
                    after()
                    at(dve.reciprocal(sig[:, :], eneg1[:, :]))
                if d.exists:
                    dve.wait_ge(S["rk"], d.n * RK + 2)
                    if d.since(2):
                        dve.wait_ge(scattered[d.par], d.pair * (16 * TOPK))
                    dve.wait_ge(S["route"], (d.n + 1) * ROUTE)
                    dve.scalar_tensor_tensor(out=pos[d.par][:, :], in0=bidxf[:, 0:TOPK], scalar=float(REGION),
                                             in1=rank[:, :], op0=ALU.mult, op1=ALU.add)\
                        .then_inc(S["pos_ready"], 1)
                if b.exists:
                    after()
                    at(dve.tensor_tensor(sfc[:, :], sig[:, :], bias_sb[:, :], ALU.add))
                if t.exists:
                    qk_products(NDH // 2, NDH)
                if b.exists:
                    after(apart=True)
                    for g in range(NGROUP):
                        at(dve.max(gtop[:, g, :], sfc[:, g * GSZ:(g + 1) * GSZ]))
                if a.exists:
                    dve.wait_ge(S["y_ready"], a.n + 1)
                    dve.wait_ge(x_loaded[a.par], a.pair * 16 + 16)
                    dve.tensor_tensor(res[:, :], x_sb[a.par][:, :], y_ps[:, 0:DM], ALU.add)\
                        .then_inc(S["res_ready"], 1)
                if b.exists:
                    after()
                    at(dve.tensor_tensor(gscore[:, 0:NGROUP], gtop[:, :, 0], gtop[:, :, 1], ALU.add))
                if a.exists:
                    dve.wait_ge(S["res_ready"], a.n + 1)
                    dve.bn_stats(stats[:, :], res[:, :]).then_inc(S["st_ready"], 1)
                if b.exists:
                    after(apart=True)
                    at(dve.max(gbest[:, :], gscore[:, :]))
                if a.exists:
                    wait_apart(dve, S["st_ready"], a.n + 1)
                    dve.bn_aggr(mv[a.par][:, :], stats[:, :]).then_inc(S["mv_ready"], 1)
                if b.exists:
                    after(apart=True)
                    at(dve.max_index(gidx[:, :], gbest[:, :], gscore[:, :]))
                if a.exists:
                    dve.wait_ge(S["mv_ready"], a.n + 1)
                    dve.tensor_scalar(veps[a.par][:, :], mv[a.par][:, 1:2], EPS, None, ALU.add)\
                        .then_inc(S["veps_ready"], 1)
                if b.exists:
                    after()
                    at(dve.tensor_copy(gidxf[:, :], gidx[:, :]))
                if t.exists:
                    dve.wait_ge(S["qk_prod_d"], t.n + 1)
                    dve.tensor_reduce(scores[:, :], prod_d.rearrange("p (s d) -> p s d", d=HD), AX, ALU.add)\
                        .then_inc(S["qk_sum_d"], 1)
                if b.exists:
                    after()
                    at(dve.tensor_scalar(gmask0[:, :], iota_e[:, 0:NGROUP], gidxf[:, 0:1], None, ALU.is_equal))
                if c.exists:
                    dve.wait_ge(S["p_ready_d"], c.n + 1)
                    dve.tensor_reduce(psum_row[:, 0:NDH], att_ps[:, 0:PD].rearrange("p (h g) -> p h g", h=NDH),
                                      AX, ALU.add).then_inc(S["p_sum"], 1)
                if b.exists:
                    after()
                    at(dve.scalar_tensor_tensor(out=gmask[:, :], in0=iota_e[:, 0:NGROUP], scalar=gidxf[:, 1:2],
                                                in1=gmask0[:, :], op0=ALU.is_equal, op1=ALU.add))
                if c.exists:
                    dve.wait_ge(S["p_ready_p"], c.n + 1)
                    dve.tensor_reduce(psum_row[:, NDH:NH], p_sb[:, :].rearrange("p (h g) -> p h g", h=NPH),
                                      AX, ALU.add).then_inc(S["p_sum"], 1)
                if b.exists:
                    after()
                    at(dve.tensor_tensor(masked[:, :].rearrange("p (g e) -> p g e", g=NGROUP),
                                         sfc[:, :].rearrange("p (g e) -> p g e", g=NGROUP),
                                         gmask[:, :].unsqueeze(2).broadcast_to([P, NGROUP, GSZ]), ALU.mult))
                if c.exists:
                    dve.wait_ge(S["p_sum"], 2 * c.n + 2)
                    dve.reciprocal(prec[:, :], psum_row[:, :]).then_inc(S["p_rec"], 1)
                if b.exists:
                    after(apart=True)
                    at(dve.max(best[:, :], masked[:, :]))
                if c.exists:
                    pv_products(0, NDH // 2)
                if b.exists:
                    after(apart=True)
                    at(dve.max_index(bidx[:, :], best[:, :], masked[:, :]))
                if c.exists:
                    pv_products(NDH // 2, NDH)
                if b.exists:
                    after()
                    at(dve.tensor_copy(bidxf[:, :], bidx[:, :]))
                if a.exists:
                    dve.wait_ge(S["rstd_ready"], a.n + 1)
                    if a.since(2):
                        dve.wait_ge(S["staged"], a.n - 1)
                    dve.tensor_scalar(x1[a.par][:, :], res[:, :], mv[a.par][:, 0:1], rstd[a.par][:, 0:1],
                                      ALU.subtract, ALU.mult).then_inc(S["x1_ready"], 1)
                if b.exists:
                    after()
                    at(dve.tensor_tensor(onehot[:, :, :],
                                         iota_e[:, :].unsqueeze(1).broadcast_to([P, TOPK, NE]),
                                         bidxf[:, 0:TOPK].unsqueeze(2).broadcast_to([P, TOPK, NE]), ALU.is_equal))
                    dve.wait_ge(S["sd_ready"], b.n + 1)
                    dve.tensor_tensor(sx[:, bass.ds(b.n * DM, DM)], x1[b.par][:, :], misc_ps[:, 0:DM], ALU.add)\
                        .then_inc(S["sx_ready"], 1)
                    after()
                    if b.since(2):
                        dve.wait_ge(S["rank_ready"], b.n - 1)
                    with nc.allow_low_precision(reason="zeros and ones"):
                        dve.tensor_reduce(picks[b.par][:, :], onehot[:, :, :].rearrange("p k e -> p e k"), AX,
                                          ALU.add).then_inc(S["picks_ready"], 1)
                    at(dve.tensor_tensor(wsel[:, :, :], onehot[:, :, :],
                                         sig[:, :].unsqueeze(1).broadcast_to([P, TOPK, NE]), ALU.mult))
                    dve.wait_ge(S["picks_ready"], 2 * b.n + 2)
                    if b.since(1):
                        dve.wait_ge(S["rank_ready"], b.n)
                    dve.tensor_tensor(seen[1 - b.par][:, :], seen[b.par][:, :], picks[b.par][:, :], ALU.add)\
                        .then_inc(S["picks_ready"], 1)
                    after()
                    at(dve.tensor_reduce(w4[:, :], wsel[:, :, :], AX, ALU.add))
                if c.exists:
                    dve.wait_ge(S["pv_prod_d"], c.n + 1)
                    dve.tensor_reduce(att[:, :], prod_d.rearrange("p (s g) -> p s g", g=NH), AX, ALU.add)\
                        .then_inc(S["pv_sum_d"], 1)
                if b.exists:
                    after()
                    at(dve.tensor_reduce(wsum[:, :], w4[:, :], AX, ALU.add))
                if t.exists:
                    dve.wait_ge(S["qk_sum_d"], t.n + 1)
                    sc_d = scores[:, :].rearrange("p (h g) -> p h g", h=NDH)
                    dve.tensor_reduce(smax[:, 0:NDH], sc_d, AX, ALU.max).then_inc(S["qk_max"], 1)
                if b.exists:
                    after()
                    at(dve.tensor_scalar(wsum1[:, :], wsum[:, :], 1e-20, None, ALU.add))
                if t.exists:
                    dve.wait_ge(S["qk_sum_p"], t.n + 1)
                    sc_p = qs_ps[t.par][:, QKS:QKS + PP].rearrange("p (h g) -> p h g", h=NPH)
                    dve.tensor_reduce(smax[:, NDH:NH], sc_p, AX, ALU.max).then_inc(S["qk_max"], 1)
                if b.exists:
                    after()
                    at(dve.reciprocal(wrec[:, :], wsum1[:, :]))
                if t.exists:
                    dve.wait_ge(S["qk_max"], 2 * t.n + 2)
                    if c.exists:
                        dve.wait_ge(S["p_ready_p"], c.n + 1)
                    dve.tensor_tensor(shifted[:, 0:PD].rearrange("p (h g) -> p h g", h=NDH), sc_d,
                                      smax[:, 0:NDH].unsqueeze(2).broadcast_to([P, NDH, NH]), ALU.subtract)\
                        .then_inc(S["qk_shift"], 1)
                    dve.tensor_tensor(shifted[:, PD:PD + PP].rearrange("p (h g) -> p h g", h=NPH), sc_p,
                                      smax[:, NDH:NH].unsqueeze(2).broadcast_to([P, NPH, NH]), ALU.subtract)\
                        .then_inc(S["qk_shift"], 1)
                if b.exists:
                    after()
                    if b.since(2):
                        dve.wait_ge(scattered[b.par], b.pair * (16 * TOPK))
                    at(dve.tensor_scalar(stage[b.par][:, :, WT], w4[:, :], wrec[:, 0:1], SCALE / 2,
                                         ALU.mult, ALU.mult))
                    at(dve.tensor_copy(stage[b.par][:, :, ID].bitcast(U32), outid[:, :]))
                    at(dve.memset(stage[b.par][:, :, WT + 1:ROW], 0.0))
                    after()
                    dve.wait_ge(S["staged"], b.n + 1)
                    at(dve.tensor_scalar(outid[:, :], outid[:, :], float(P), None, ALU.add))
                    assert done[0] == ROUTE

            each_step(dve, 0, NT + 3, 1, 4, step)

            steps = [0]

            def at(ins):
                steps[0] += 1
                return ins.then_inc(S["b"], 1)

            def after():
                dve.wait_ge(S["b"], steps[0])

            dve.wait_ge(S["count_ready"], 1)
            at(dve.tensor_scalar(cnt_u[:, :], misc_ps[:, 0:NE], float(P - 1), None, ALU.add))
            after()
            at(dve.tensor_scalar(ntile_u[:, :], cnt_u[:, :], 7, None, ALU.logical_shift_right))
            after()
            at(dve.tensor_copy(ntile[:, :], ntile_u[:, :]))
            after()
            at(dve.tensor_tensor_scan(tend[:, :], ones_e[:, :], ntile[:, :], 0.0, ALU.mult, ALU.add))
            after()
            for c in range(2):
                at(dve.tensor_scalar(past[:, c, :], tend[:, :], slot_col[:, c:c + 1], None, ALU.is_le))
            after()
            at(dve.tensor_reduce(slot_e[:, :], past[:, :, :], AX, ALU.add))
            at(dve.tensor_tensor(pend[:, :, :], past[:, :, :],
                                 tend[:, :].unsqueeze(1).broadcast_to([P, 2, NE]), ALU.mult))
            after()
            at(dve.tensor_reduce(slot_first[:, :], pend[:, :, :], AX, ALU.max))
            after()
            at(dve.tensor_tensor(slot_k[:, :], slot_col[:, :], slot_first[:, :], ALU.subtract))
            after()
            at(dve.tensor_scalar(slot_k[:, :], slot_k[:, :], float(P), None, ALU.mult))
            after()
            at(dve.scalar_tensor_tensor(out=slot_row[:, 0:2], in0=slot_e[:, :], scalar=float(REGION),
                                        in1=slot_k[:, :], op0=ALU.mult, op1=ALU.add))
            at(dve.tensor_scalar(slot_row[:, 2:4], slot_e[:, :], float(NE - 1), float(KC * 2 * EI),
                                 ALU.min, ALU.mult))
            assert steps[0] == BSTEPS
            dve.wait_ge(S["tabT"], 1)
            at(dve.tensor_copy(tab[0:1, 0:2 * SLOTS], tr_ps[0:1, 0:2 * SLOTS]))
            at(dve.tensor_tensor(tab[0:1, 2 * SLOTS:2 * SLOTS + NE], region0[0:1, :], misc_ps[0:1, 0:NE], ALU.add))
            at(dve.tensor_scalar(quadf[:, :], tend[:, NE - 1:NE], float(QUAD - 1 - 2 * QUAD), None, ALU.add))
            after()
            at(dve.tensor_scalar(tab[0:1, QUADS:QUADS + 1].bitcast(U32), quadf[0:1, :], 2, None,
                                 ALU.logical_shift_right))
            after()
            dve.memset(quadf[:, :], 0.0).then_inc(S["tab_ready"], 1)

            quads = n_quads(dve)

            def copy_meta(n, par, quad):
                dve.wait_ge(xt_loaded[par], quad * 32 + 32)
                if not (isinstance(n, int) and n < 2):
                    dve.wait_ge(S["ids_ready"], n - 1)
                dve.tensor_copy(meta[par][:, :, :], xt[par][:, :, ID:ID + 2]).then_inc(S["cmeta"], 1)

            def pairs(quad, par, has_prev, has_next):
                n = quad * 2 + par
                if has_next:
                    copy_meta(n + 1, 1 - par, quad + par)
                g_u = banks[par][:, :].rearrange("p (j f) -> p j f", j=2)
                dve.wait_ge(S["cth_ready"], n + 1)
                dve.scalar_tensor_tensor(out=cgth[:, :, :], in0=cth[par][:, :, :], scalar=1.0,
                                         in1=g_u[:, :, 0:EI], op0=ALU.add, op1=ALU.mult)\
                    .then_inc(S["cgth_ready"], 1)
                dve.wait_ge(S["cgth_ready"], n + 1)
                dve.wait_ge(S["cmeta"], n + 1)
                if has_prev:
                    dve.wait_ge(S["chT_ps"], n)
                for j in range(2):
                    dve.scalar_tensor_tensor(out=ch[:, j, :], in0=cgth[:, j, :], scalar=meta[par][:, j, 1:2],
                                             in1=g_u[:, j, EI:2 * EI], op0=ALU.mult, op1=ALU.mult)\
                        .then_inc(S["ch_ready"], 1)
                dve.wait_ge(S["chT_ps"], n + 1)
                if has_prev:
                    dve.wait_ge(S["cy_ps"], n)
                dve.tensor_copy(chT[:, :], banks[3][:, 0:2 * P]).then_inc(S["chT_copied"], 1)
                if not (isinstance(n, int) and n < 2):
                    dve.wait_ge(y_scattered[par], quad * 32)
                dve.tensor_copy(ids[par][:, :], meta[par][:, :, 0].bitcast(U32)).then_inc(S["ids_ready"], 1)

            copy_meta(0, 0, 0)
            quads_with_ends(dve, quads, pairs)

            def dstep(t):
                a, b = t.ago(1), t.ago(2)
                if t.exists:
                    dve.wait_ge(z_loaded[t.par], t.pair * 16 + 16)
                    if t.since(2):
                        dve.wait_ge(S["d_ps"], t.n - 1)
                    dve.tensor_tensor(z2[t.par][:, :, :], zt[t.par][:, 0:2, :], zt[t.par][:, 2:4, :], ALU.add)\
                        .then_inc(S["d_a"], 1)
                if b.exists:
                    dve.wait_ge(S["drstd_ready"], b.n + 1)
                    if b.since(2):
                        dve.wait_ge(stored[b.par], b.pair * 16)
                    dve.tensor_scalar(o2[b.par][:, :], banks[b.par][:, 0:DM], mv[b.par][:, 0:1],
                                      rstd[b.par][:, 0:1], ALU.subtract, ALU.mult)\
                        .then_inc(S["o2_ready"], 1)
                if a.exists:
                    dve.wait_ge(S["d_ps"], a.n + 1)
                    dve.bn_stats(stats[:, :], banks[a.par][:, 0:DM]).then_inc(S["dst_ready"], 1)
                    wait_apart(dve, S["dst_ready"], a.n + 1)
                    dve.bn_aggr(mv[a.par][:, :], stats[:, :]).then_inc(S["dmv_ready"], 1)
                    dve.wait_ge(S["dmv_ready"], a.n + 1)
                    dve.tensor_scalar(veps[a.par][:, :], mv[a.par][:, 1:2], EPS, None, ALU.add)\
                        .then_inc(S["dveps_ready"], 1)

            each_step(dve, 0, NT + 1, 0, 2, dstep)


ROUTE = 27
RK = 2
BSTEPS = 13


def kernel(L0_attn_x, L0_attn_Wq, L0_attn_Wk, L0_attn_Wv, L0_attn_Wfc, L0_ffn_router_weight,
           L0_ffn_router_bias, L0_ffn_gate_w, L0_ffn_up_w, L0_ffn_down_w, L0_ffn_shared_gate_w,
           L0_ffn_shared_up_w, L0_ffn_shared_down_w):
    import numpy as np
    import concourse.bacc as bacc
    from concourse.bass_utils import run_bass_kernel_spmd

    def arr(a):
        return np.asarray(a)

    def chunked(w):
        w = arr(w)
        return np.ascontiguousarray(w.reshape(w.shape[0], -1, P).transpose(2, 1, 0))

    x = arr(L0_attn_x).reshape(NTOK, DM)
    wv = arr(L0_attn_Wv).reshape(NH, HD, DM).transpose(1, 0, 2).reshape(DM, DM)
    gate = arr(L0_ffn_gate_w).reshape(NE, EI, KC, P)
    up = arr(L0_ffn_up_w).reshape(NE, EI, KC, P)
    ins = {
        "xT": x.reshape(NT, P, KC, P).transpose(0, 3, 2, 1).reshape(NTOK, DM),
        "x": x,
        "wqkv": chunked(np.concatenate([arr(L0_attn_Wq), arr(L0_attn_Wk), wv], axis=0)),
        "wfc": chunked(L0_attn_Wfc),
        "wr": chunked(L0_ffn_router_weight),
        "rbias": np.broadcast_to(arr(L0_ffn_router_bias)[None, :], (P, NE)),
        "wsgu": chunked(np.concatenate([arr(L0_ffn_shared_gate_w), arr(L0_ffn_shared_up_w)], axis=0)),
        "wsd": chunked(L0_ffn_shared_down_w),
        "wgu": np.concatenate([gate, up], axis=1).transpose(3, 0, 2, 1).reshape(P, -1),
        "wd": arr(L0_ffn_down_w).transpose(2, 0, 1).reshape(P, -1),
    }
    nc = bacc.Bacc("TRN2", target_bir_lowering=False, num_devices=1)
    arrays, args = {}, []
    for name, a in ins.items():
        a = np.ascontiguousarray(a)
        arrays[f"in_{name}"] = a
        args.append(nc.dram_tensor(f"in_{name}", a.shape, mybir.dt.from_np(a.dtype), kind="ExternalInput").ap())
    args.append(nc.dram_tensor("out_0", (NTOK, DM), F32, kind="ExternalOutput").ap())
    build(nc, *args)
    r = run_bass_kernel_spmd(nc, [arrays], core_ids=[0])
    return r.results[0]["out_0"].reshape(4, NTOK // 4, DM)
```

```python
from contextlib import ExitStack

import concourse.bass as bass
from concourse import mybir

F32 = mybir.dt.float32
BF16 = mybir.dt.bfloat16
U32 = mybir.dt.uint32
I32 = mybir.dt.int32
ALU = mybir.AluOpType
ACT = mybir.ActivationFunctionType
AX = mybir.AxisListType.X

P = 128
NTOK, DM = 4096, 256
NT = NTOK // P
KC = DM // P
NH = 16
HD = DM // NH
NE, EI = 32, 128
TOPK, NGROUP = 4, 4
GSZ = NE // NGROUP
SHI = 256
SCALE = 2.5
NPH = 9
NDH = NH - NPH
HW = NH * HD
PD = NDH * NH
PP = NPH * NH
NVS = NDH + 1
NTS = NH - NVS
VS = NVS * NH
TS = NTS * NH
EPS = 1e-5
ROW = DM + 8
ID, WT = DM, DM + 1
FILL_ACT, FILL_SP = 10, 20
WD_FIRST = NE - NPH * HW // DM
QUAD = 4
MAXTILES = NTOK * TOPK // P + NE - 1
EBITS = 5
assert NE == 1 << EBITS
SLOTS = 2 * P
PADS = SLOTS + SLOTS // QUAD
REGION = NTOK + P
XROWS = NE * REGION + QUAD * P
NOWHERE = 1 << 18
assert MAXTILES + QUAD <= SLOTS


class Tile:

    def __init__(self, pair, par, ways=2):
        self.pair, self.par, self.ways, self.n = pair, par, ways, pair * ways + par

    def ago(self, k):
        q = self.par - k
        return Tile(self.pair + q // self.ways, q % self.ways, self.ways)

    @property
    def exists(self):
        return not isinstance(self.n, int) or 0 <= self.n < NT

    def since(self, k):
        return not isinstance(self.n, int) or self.n >= k


def each_step(eng, first, last, lead, lag, body, ways=2, unroll=2):
    size = ways * unroll
    lo = -(-(lag + ways) // size) * size
    hi = (NT - lead) // size * size
    for s in range(first, lo):
        body(Tile(s // ways, s % ways, ways))
    with eng.Fori(lo // size, hi // size) as block:
        for s in range(size):
            body(Tile(block * unroll + s // ways, s % ways, ways))
    for s in range(hi, last + 1):
        body(Tile(s // ways, s % ways, ways))


def build(nc, xT, x, wqkv, wfc, wr, rbias, wsgu, wsd, wgu, wd, out):
    xs = nc.dram_tensor("expert_rows", [XROWS, ROW], F32).ap()
    z = nc.dram_tensor("pick_rows", [TOPK * NTOK, DM], F32).ap()

    with ExitStack() as ctx:
        def sb(name, shape, dt=F32):
            return ctx.enter_context(nc.sbuf_tensor(name, shape, dt))

        def bank(name):
            return ctx.enter_context(nc.psum_tensor(name, [P, 512], F32))

        def sem(name):
            return ctx.enter_context(nc.semaphore(name))

        wqkv_sb = sb("wqkv_sb", [P, KC, 3 * DM])
        wfc_sb = sb("wfc_sb", [P, KC, DM])
        wr_sb = sb("wr_sb", [P, KC, NE])
        bias_sb = sb("bias_sb", [P, NE])
        wsgu_sb = sb("wsgu_sb", [P, KC, 2 * SHI])
        wsd_sb = sb("wsd_sb", [P, SHI // P, DM])
        wgu_sb = sb("wgu_sb", [P, NE * KC * 2 * EI])
        wd_sb = sb("wd_sb", [P, NE * DM])
        ident = sb("ident", [P, P])
        before_b = sb("before_b", [P, P], BF16)
        rest_b = sb("rest_b", [P, P], BF16)
        iota_e = sb("iota_e", [P, NE])
        slot_col = sb("slot_col", [P, 2])
        neg_half = sb("neg_half", [P, 1])
        pad_rows = sb("pad_rows", [P, ROW])
        xT_sb = [sb(f"xT_sb{i}", [P, KC, P]) for i in range(2)]
        x_sb = [sb(f"x_sb{i}", [P, DM]) for i in range(2)]
        k_sb = [sb(f"k_sb{i}", [P, DM]) for i in range(2)]
        v_sb = [sb(f"v_sb{i}", [P, DM]) for i in range(2)]
        q_sb = [sb(f"q_sb{i}", [P, NPH * HD]) for i in range(2)]
        prod = sb("prod", [P, (NDH + 2 * NPH) * HW])
        prod_d = prod[:, 0:NDH * HW]
        prod_q = [prod[:, NDH * HW:NH * HW], wd_sb[:, WD_FIRST * DM:NE * DM]]
        prod_p = prod[:, NH * HW:(NH + NPH) * HW]
        scores = sb("scores", [P, VS])
        smax = sb("smax", [P, NH])
        shifted = sb("shifted", [P, NH * NH])
        psum_row = sb("psum_row", [P, NH])
        prec = sb("prec", [P, NH])
        p_sb = sb("p_sb", [P, PP])
        att = sb("att", [P, NDH * HD])
        o_sb = sb("o_sb", [P, DM])
        ohT_sb = sb("ohT_sb", [P, KC + SHI // P, P])
        res = sb("res", [P, DM])
        eps_col = sb("eps_col", [P, 1])
        rsum = sb("rsum", [P, 1])
        rsquare = sb("rsquare", [P, 1])
        nmean = sb("nmean", [P, 1])
        nmr = sb("nmr", [P, 1])
        stats = sb("stats", [P, 6])
        mv = [sb(f"mv{i}", [P, 2]) for i in range(4)]
        veps = [sb(f"veps{i}", [P, 1]) for i in range(4)]
        rstd = [sb(f"rstd{i}", [P, 1]) for i in range(4)]
        x1 = [sb(f"x1_{i}", [P, DM]) for i in range(2)]
        x1T_sb = sb("x1T_sb", [P, KC, P])
        th_sb = sb("th_sb", [P, SHI])
        gth_sb = sb("gth_sb", [P, SHI])
        hs_sb = sb("hs_sb", [P, SHI])
        sx = sb("sx", [P, NT * DM])
        eneg = sb("eneg", [P, NE])
        eneg1 = sb("eneg1", [P, NE])
        sig = sb("sig", [P, NE])
        sfc = sb("sfc", [P, NE])
        gtop = sb("gtop", [P, NGROUP, 8])
        gscore = sb("gscore", [P, 8])
        gbest = sb("gbest", [P, 8])
        gidx = sb("gidx", [P, 8], U32)
        gmask2 = sb("gmask2", [P, 2, NGROUP])
        gmask = sb("gmask", [P, NGROUP])
        masked = sb("masked", [P, NE])
        best = sb("best", [P, 8])
        bidx = sb("bidx", [P, 8], U32)
        onehot = [sb(f"onehot{i}", [P, TOPK, NE], BF16) for i in range(2)]
        wsel = sb("wsel", [P, TOPK, NE])
        w4 = sb("w4", [P, TOPK])
        wsum = sb("wsum", [P, 1])
        wsum1 = sb("wsum1", [P, 1])
        wrec = sb("wrec", [P, 1])
        rsel = sb("rsel", [P, TOPK, NE])
        ranks_sb = sb("ranks_sb", [P, NE])
        rank = sb("rank", [P, TOPK])
        pos = [sb(f"pos{i}", [P, TOPK], U32) for i in range(2)]
        outid = [sb(f"outid{i}", [P, TOPK]) for i in range(2)]
        tile_step = sb("tile_step", [P, 1])
        stage = [sb(f"stage{i}", [P, TOPK, ROW]) for i in range(2)]
        cnt_u = sb("cnt_u", [P, NE], U32)
        ntile_u = sb("ntile_u", [P, NE], U32)
        ntile = sb("ntile", [P, NE])
        ones_e = sb("ones_e", [P, NE])
        tend = sb("tend", [P, NE])
        past = sb("past", [P, 2, NE])
        pend = sb("pend", [P, 2, NE])
        slot_e = sb("slot_e", [P, 2])
        slot_first = sb("slot_first", [P, 2])
        slot_k = sb("slot_k", [P, 2])
        slot_row = sb("slot_row", [P, 4])
        region0 = sb("region0", [P, NE])
        tab = sb("tab", [1, PADS + NE + 8], I32)
        pack = [sb(f"pack{i}", [1, SLOTS // QUAD]) for i in range(2)]
        packed = sb("packed", [1, SLOTS // QUAD], U32)
        before = sb("before", [1, SLOTS // QUAD], U32)
        quadf = sb("quadf", [P, 1], U32)
        ids = [sb(f"ids{i}", [P, 2], U32) for i in range(2)]
        meta = [sb(f"meta{i}", [P, 2, 2]) for i in range(2)]
        def over_prod(at, *shape):
            size = 1
            for s in shape:
                size *= s
            part = prod[:, at:at + size]
            return part.rearrange("p (a b) -> p a b", a=shape[0]) if len(shape) > 1 else part

        xtT = [over_prod(i * 2 * DM, 2 * KC * P) for i in range(2)]
        chT = over_prod(4 * DM, 2 * P)
        y_sb = [over_prod((5 + 2 * i) * DM, 2, DM) for i in range(2)]
        xt = [over_prod(9 * DM + i * 2 * ROW, 2, ROW) for i in range(2)]
        cth = [over_prod(9 * DM + 4 * ROW + i * 2 * EI, 2, EI) for i in range(2)]
        cgth = over_prod(9 * DM + 4 * ROW + 4 * EI, 2, EI)
        ch = over_prod(9 * DM + 4 * ROW + 6 * EI, 2, EI)
        DWAYS = 4

        def over_wgu(at, rows):
            return wgu_sb[:, at * DM:(at + rows) * DM].rearrange("p (a b) -> p a b", a=rows)

        zt = [over_wgu(i * TOPK, TOPK) for i in range(DWAYS)]
        z2 = [over_wgu(DWAYS * TOPK + i * 2, 2) for i in range(DWAYS)]
        o2 = [wgu_sb[:, (DWAYS * (TOPK + 2) + i) * DM:(DWAYS * (TOPK + 2) + i + 1) * DM] for i in range(DWAYS)]

        banks = [bank(f"bank{i}") for i in range(8)]
        qs_ps = banks[0:2]
        QKS = DM
        kv_ps = banks[2]
        tr_ps = banks[3]
        y_ps = banks[4]
        gu_ps = banks[5]
        att_ps = banks[6]
        PVS = PD
        misc_ps = banks[7]

        SEMS = """xT_loaded0 xT_loaded1 x_loaded0 x_loaded1 qkv_w small_w big_w consts pads cast
        q_ready kv_ready q_copied k_copied v_copied qk_prod_d qk_prod_p qk_sum_d qk_sum_x qk_sum_p qk_max qk_shift
        p_ready_d p_ready_p p_sum p_rec pv_prod_d pv_prod_p pv_sum_d pv_sum_p att_ready
        ohT_ps ohT_copied y_ready res_ready st_ready nmean_ready nmr_ready veps_ready rstd_ready x1_ready staged outid_ready
        x1T_ps x1T_copied logits_ready gu_ready eneg_ready th_ready gth_ready hs_ready
        sd_ready sx_ready route rank_ready rk pos_ready scat0 scat1
        b tabT tab_ready filled_act filled_sp filled_pool
        xt0 xt1 cX_ps cX_copied cmeta ids_ready cgu_ps cth_ready cgth_ready ch_ready chT_ps chT_copied cy_ps cy_copied
        yscat0 yscat1
        z_loaded0 z_loaded1 z_loaded2 z_loaded3 d_a d_ps dst_ready dmv_ready dveps_ready drstd_ready o2_ready
        stored0 stored1 stored2 stored3""".split()
        S = {name: sem(name) for name in SEMS}
        xT_loaded = [S["xT_loaded0"], S["xT_loaded1"]]
        x_loaded = [S["x_loaded0"], S["x_loaded1"]]
        scattered = [S["scat0"], S["scat1"]]
        xt_loaded = [S["xt0"], S["xt1"]]
        y_scattered = [S["yscat0"], S["yscat1"]]
        z_loaded = [S[f"z_loaded{i}"] for i in range(4)]
        stored = [S[f"stored{i}"] for i in range(4)]

        NSMALL = 5 * 16
        QUADS = PADS + NE

        block = ctx.enter_context(nc.Block())

        def wait_apart(eng, semaphore, value):
            goal = value if isinstance(value, int) else eng.snap(eng.to_reg(value))
            eng.wait_ge(S["consts"], 15)
            eng.wait_ge(semaphore, goal)

        def n_quads(eng):
            eng.wait_ge(S["tab_ready"], 1)
            return eng.value_load(tab[0:1, QUADS:QUADS + 1], min_val=NTOK * TOPK // P // QUAD - 2,
                                  max_val=(MAXTILES + QUAD - 1) // QUAD - 2) + 2

        def fill_padding(eng, first, last, filled):
            with eng.Fori(first, last) as e:
                row = eng.value_load(tab[0:1, bass.ds(e + PADS, 1)], min_val=0, max_val=XROWS - P)
                eng.dma_start(xs[bass.ds(row, P), :], pad_rows[:, :]).then_inc(filled, 16)

        @block.sync
        def _(sp):
            sp.dma_start(wqkv_sb[:, :, :], wqkv).then_inc(S["qkv_w"], 16)

            def load_xT(t):
                if t.since(2):
                    sp.wait_ge(S["kv_ready"], t.n - 1)
                sp.dma_start(xT_sb[t.par][:, :, :], xT[bass.ds(t.n * P, P), :]).then_inc(xT_loaded[t.par], 16)

            def load_expert(e):
                width = KC * 2 * EI
                sp.dma_start(wgu_sb[:, bass.ds(e * width, width)], wgu[:, bass.ds(e * width, width)])\
                    .then_inc(S["big_w"], 16)

            def load_x(t):
                if t.since(2):
                    sp.wait_ge(S["res_ready"], t.n - 1)
                sp.dma_start(x_sb[t.par][:, :], x[bass.ds(t.n * P, P), :]).then_inc(x_loaded[t.par], 16)

            def step(t):
                b = t.ago(3)
                if t.exists:
                    load_xT(t)
                if b.exists:
                    load_x(b)
                    load_expert(b.n)

            step(Tile(0, 0))
            step(Tile(0, 1))
            for dst, src in ((wfc_sb[:, :, :], wfc), (wr_sb[:, :, :], wr), (wsgu_sb[:, :, :], wsgu),
                             (wsd_sb[:, :, :], wsd), (bias_sb[:, :], rbias)):
                sp.dma_start(dst, src).then_inc(S["small_w"], 16)
            sp.dma_start(wd_sb[:, 0:WD_FIRST * DM], wd[:, 0:WD_FIRST * DM]).then_inc(S["big_w"], 16)
            each_step(sp, 2, NT + 2, 0, 3, step)
            sp.wait_ge(S["qk_sum_p"], NT)
            sp.wait_ge(S["qk_sum_x"], NT)
            sp.dma_start(wd_sb[:, WD_FIRST * DM:NE * DM], wd[:, WD_FIRST * DM:NE * DM])\
                .then_inc(S["big_w"], 16)

            quads = n_quads(sp)
            fill_padding(sp, FILL_ACT, FILL_SP, S["filled_sp"])
            for par in range(2):
                sp.wait_ge(scattered[par], 16 * TOPK * (NT // 2))
            sp.wait_ge(S["filled_act"], 16 * FILL_ACT)
            sp.wait_ge(S["filled_sp"], 16 * (FILL_SP - FILL_ACT))
            sp.wait_ge(S["filled_pool"], 16 * (NE - FILL_SP))
            sp.wait_ge(S["pads"], 16 * QUAD)

            def load_rows(pair, par, first):
                if not first:
                    sp.wait_ge(S["cX_ps"], 2 * pair + par - 1)
                    sp.wait_ge(S["cmeta"], 2 * pair + par - 1)
                for j in range(2):
                    row = sp.value_load(tab[0:1, bass.ds(pair * QUAD + 2 * par + j, 1)],
                                        min_val=0, max_val=XROWS - P)
                    sp.dma_start(xt[par][:, j, :], xs[bass.ds(row, P), :]).then_inc(xt_loaded[par], 16)

            load_rows(0, 0, True)
            load_rows(0, 1, True)
            with sp.Fori(1, quads) as quad:
                load_rows(quad, 0, False)
                load_rows(quad, 1, False)

            for par in range(2):
                sp.wait_ge(y_scattered[par], quads * 32)

            def load_z(t):
                if t.since(DWAYS):
                    sp.wait_ge(S["d_a"], t.n - (DWAYS - 1))
                sp.dma_start(zt[t.par][:, :, :],
                             z.rearrange("(k n) c -> n k c", k=TOPK)[bass.ds(t.n * P, P), :, :])\
                    .then_inc(z_loaded[t.par], 16)

            each_step(sp, 0, NT - 1, 0, 0, load_z, DWAYS, 1)

        @block.gpsimd
        def _(pool):
            pool.memset(ident[:, :], 1.0).then_inc(S["consts"], 1)
            pool.memset(before_b[:, :], 1.0).then_inc(S["consts"], 1)
            pool.memset(rest_b[:, :], 1.0).then_inc(S["consts"], 1)
            pool.memset(neg_half[:, :], -0.5).then_inc(S["consts"], 1)
            pool.memset(pad_rows[:, :], 0.0).then_inc(S["consts"], 1)
            pool.iota(iota_e[:, :], [[1, NE]], base=0, channel_multiplier=0,
                      allow_small_or_imprecise_dtypes=True).then_inc(S["consts"], 1)
            pool.iota(slot_col[:, :], [[P, 2]], base=0, channel_multiplier=1,
                      allow_small_or_imprecise_dtypes=True).then_inc(S["consts"], 1)
            pool.iota(region0[:, :], [[REGION, NE]], base=0, channel_multiplier=0,
                      allow_small_or_imprecise_dtypes=True).then_inc(S["consts"], 1)
            pool.iota(outid[0][:, :], [[NTOK, TOPK]], base=0, channel_multiplier=1,
                      allow_small_or_imprecise_dtypes=True).then_inc(S["consts"], 1)
            pool.wait_ge(S["consts"], 9)
            pool.affine_select(out=ident[:, :], in_=ident[:, :], compare_op=ALU.is_equal, fill=0.0,
                               base=0, pattern=[[-1, P]], channel_multiplier=1).then_inc(S["consts"], 1)
            pool.affine_select(out=before_b[:, :], in_=before_b[:, :], compare_op=ALU.is_gt, fill=0.0,
                               base=0, pattern=[[1, P]], channel_multiplier=-1).then_inc(S["consts"], 1)
            pool.affine_select(out=rest_b[:, :], in_=rest_b[:, :], compare_op=ALU.is_ge, fill=0.0,
                               base=0, pattern=[[-1, P]], channel_multiplier=1).then_inc(S["consts"], 1)
            pool.iota(pad_rows[:, ID:ID + 1], [[0, 1]], base=NOWHERE, channel_multiplier=1,
                      allow_small_or_imprecise_dtypes=True).then_inc(S["consts"], 1)
            pool.memset(tile_step[:, :], float(P)).then_inc(S["consts"], 1)
            pool.memset(eps_col[:, :], EPS).then_inc(S["consts"], 1)

            def pv_part(c, g0, g1):
                n = g1 - g0
                return pool.tensor_tensor(
                    prod_p[:, g0 * PP:g1 * PP].rearrange("p (g h d) -> p g h d", g=n, h=NPH),
                    p_sb[:, :].rearrange("p (h g o) -> p g h o", h=NPH, o=1)[:, g0:g1].broadcast_to([P, n, NPH, HD]),
                    v_sb[c.par][:, :].rearrange("p (d g o) -> p g o d", g=NH, o=1)[:, g0:g1]
                    .broadcast_to([P, n, NPH, HD]), ALU.mult)

            def scatter_rows(d):
                wait_apart(pool, S["pos_ready"], d.n + 1)
                for k in range(TOPK):
                    pool.indirect_dma_start(
                        xs, bass.IndirectOffsetOnAxis(ap=pos[d.par][:, k:k + 1], axis=0),
                        stage[d.par][:, k, :], None, bounds_check=XROWS - 1,
                        oob_is_err=False).then_inc(scattered[d.par], 16)

            def step(t):
                c, a, d = t.ago(1), t.ago(2), t.ago(4)
                if t.exists:
                    if t.since(2):
                        pool.wait_ge(S["qk_sum_p"], t.n - 1)
                        pool.wait_ge(S["qk_sum_x"], t.n - 1)
                    pool.wait_ge(S["q_copied"], t.n + 1)
                    pool.wait_ge(S["k_copied"], t.n + 1)
                    pool.tensor_tensor(
                        prod_q[t.par].rearrange("p (d h g) -> p d h g", d=HD, h=NPH),
                        q_sb[t.par][:, :].rearrange("p (h d o) -> p d h o", h=NPH, o=1).broadcast_to([P, HD, NPH, NH]),
                        k_sb[t.par][:, :].rearrange("p (g d o) -> p d o g", g=NH, o=1).broadcast_to([P, HD, NPH, NH]),
                        ALU.mult).then_inc(S["qk_prod_p"], 1)
                if d.exists:
                    scatter_rows(d)
                if c.exists:
                    if c.since(1):
                        pool.wait_ge(S["pv_sum_p"], c.n)
                    pool.wait_ge(S["p_ready_p"], c.n + 1)
                    pool.wait_ge(S["v_copied"], c.n + 1)
                    pv_part(c, 0, NH // 2)
                if a.exists:
                    pool.wait_ge(S["veps_ready"], a.n + 1)
                    pool.tensor_tensor(rstd[a.par][:, :], veps[a.par][:, :], neg_half[:, :], ALU.pow)\
                        .then_inc(S["rstd_ready"], 1)
                if c.exists:
                    pv_part(c, NH // 2, NH).then_inc(S["pv_prod_p"], 1)

            each_step(pool, 0, NT + 3, 0, 4, step)

            quads = n_quads(pool)
            fill_padding(pool, FILL_SP, NE, S["filled_pool"])

            def scatter_y(pair, par):
                wait_apart(pool, S["ids_ready"], pair * 2 + par + 1)
                wait_apart(pool, S["cy_copied"], pair * 2 + par + 1)
                for j in range(2):
                    pool.indirect_dma_start(
                        z, bass.IndirectOffsetOnAxis(ap=ids[par][:, j:j + 1], axis=0),
                        y_sb[par][:, j, :], None, bounds_check=TOPK * NTOK - 1,
                        oob_is_err=False).then_inc(y_scattered[par], 16)

            with pool.Fori(0, quads) as quad:
                scatter_y(quad, 0)
                scatter_y(quad, 1)

            with pool.Fori(0, NT // DWAYS) as group:
                for par in range(DWAYS):
                    pool.wait_ge(S["dveps_ready"], group * DWAYS + (par + 1))
                    pool.tensor_tensor(rstd[par][:, :], veps[par][:, :], neg_half[:, :], ALU.pow)\
                        .then_inc(S["drstd_ready"], 1)

        def quads_with_ends(eng, quads, body):
            body(0, 0, False, True)
            body(0, 1, True, True)
            with eng.Fori(1, quads - 1) as quad:
                body(quad, 0, True, True)
                body(quad, 1, True, True)
            body(quads - 1, 0, True, True)
            body(quads - 1, 1, True, False)

        @block.scalar
        def _(act):
            act.wait_ge(S["consts"], 15)
            for i in range(QUAD):
                act.dma_start(xs[NE * REGION + i * P:NE * REGION + (i + 1) * P, :], pad_rows[:, :])\
                    .then_inc(S["pads"], 16)

            def copy_q(t):
                act.wait_ge(S["q_ready"], t.n + 1)
                if t.since(2):
                    act.wait_ge(S["qk_prod_p"], t.n - 1)
                act.activation(q_sb[t.par][:, :], qs_ps[t.par][:, NDH * HD:DM], ACT.Copy)\
                    .then_inc(S["q_copied"], 1)

            def copy_k(t):
                act.wait_ge(S["kv_ready"], t.n + 1)
                if t.since(2):
                    act.wait_ge(S["qk_prod_p"], t.n - 1)
                    act.wait_ge(S["qk_prod_d"], t.n - 1)
                act.activation(k_sb[t.par][:, :], kv_ps[:, 0:DM], ACT.Copy).then_inc(S["k_copied"], 1)

            def step(t):
                c, a, b = t.ago(1), t.ago(2), t.ago(3)
                if t.exists:
                    act.wait_ge(S["kv_ready"], t.n + 1)
                    if t.since(2):
                        act.wait_ge(S["pv_prod_d"], t.n - 1)
                        act.wait_ge(S["pv_prod_p"], t.n - 1)
                    act.activation(v_sb[t.par][:, :], kv_ps[:, DM:2 * DM], ACT.Copy).then_inc(S["v_copied"], 1)
                if c.exists:
                    act.wait_ge(S["qk_shift"], 2 * c.n + 2)
                    if a.exists:
                        act.wait_ge(S["pv_prod_d"], a.n + 1)
                        act.wait_ge(S["p_sum"], 2 * a.n + 2)
                        act.wait_ge(S["att_ready"], 2 * a.n + 2)
                    act.activation(att_ps[:, 0:PD], shifted[:, 0:PD], ACT.Exp, scale=HD ** -0.5)\
                        .then_inc(S["p_ready_d"], 1)
                if a.exists or b.exists:
                    act.wait_ge(S["ohT_ps"], t.n - 1)
                    lo, hi = 0 if a.exists else KC, KC + SHI // P if b.exists else KC
                    act.activation(ohT_sb[:, lo:hi, :], tr_ps[:, lo * P:hi * P], ACT.Copy)\
                        .then_inc(S["ohT_copied"], 1)
                if t.ago(-1).exists:
                    copy_q(t.ago(-1))
                if b.exists:
                    if b.since(2):
                        act.wait_ge(scattered[b.par], b.pair * (16 * TOPK))
                    act.wait_ge(S["x1_ready"], b.n + 1)
                    act.activation(stage[b.par][:, :, 0:DM],
                                   x1[b.par][:, :].unsqueeze(1).broadcast_to([P, TOPK, DM]), ACT.Copy)
                    if b.since(1):
                        act.wait_ge(S["outid_ready"], b.n)
                    act.activation(stage[b.par][:, :, ID], outid[b.par][:, :], ACT.Copy).then_inc(S["staged"], 1)
                    act.activation(outid[1 - b.par][:, :], outid[b.par][:, :], ACT.Identity,
                                   bias=tile_step[:, 0:1]).then_inc(S["outid_ready"], 1)
                if a.exists:
                    act.wait_ge(S["res_ready"], a.n + 1)
                    if a.since(2):
                        act.wait_ge(S["staged"], a.n - 1)
                        act.wait_ge(S["sx_ready"], a.n - 1)
                    act.activation(x1[a.par][:, :], res[:, :], ACT.Copy, accum_out=rsum[:, :]).then_inc(S["st_ready"], 1)
                    act.wait_ge(S["st_ready"], 2 * a.n + 1)
                    act.activation(nmean[:, :], rsum[:, :], ACT.Copy, scale=-1.0 / DM).then_inc(S["nmean_ready"], 1)
                    act.wait_ge(S["nmean_ready"], a.n + 1)
                    act.activation(x1[a.par][:, :], res[:, :], ACT.Square, bias=nmean[:, 0:1],
                                   accum_out=rsquare[:, :]).then_inc(S["st_ready"], 1)
                    act.wait_ge(S["st_ready"], 2 * a.n + 2)
                    act.activation(veps[a.par][:, :], rsquare[:, :], ACT.Identity, bias=eps_col[:, 0:1],
                                   scale=1.0 / DM).then_inc(S["veps_ready"], 1)
                    act.wait_ge(S["rstd_ready"], a.n + 1)
                    act.activation(nmr[:, :], nmean[:, :], ACT.Copy, scale=rstd[a.par][:, 0:1])\
                        .then_inc(S["nmr_ready"], 1)
                    act.wait_ge(S["nmr_ready"], a.n + 1)
                    act.activation(x1[a.par][:, :], res[:, :], ACT.Identity, bias=nmr[:, 0:1],
                                   scale=rstd[a.par][:, 0:1]).then_inc(S["x1_ready"], 1)
                if t.ago(-1).exists:
                    copy_k(t.ago(-1))
                if a.exists:
                    act.wait_ge(S["x1T_ps"], a.n + 1)
                    act.activation(x1T_sb[:, :, :], tr_ps[:, 0:DM], ACT.Copy).then_inc(S["x1T_copied"], 1)
                if a.exists:
                    act.wait_ge(S["logits_ready"], a.n + 1)
                    if a.since(1):
                        act.wait_ge(S["route"], a.n * ROUTE - (ROUTE - 1))
                    act.activation(eneg[:, :], y_ps[:, DM:DM + NE], ACT.Exp, scale=-1.0)\
                        .then_inc(S["eneg_ready"], 1)
                    act.wait_ge(S["gu_ready"], a.n + 1)
                    act.activation(th_sb[:, :], gu_ps[:, 0:SHI], ACT.Tanh, scale=0.5)\
                        .then_inc(S["th_ready"], 1)
                if t.exists:
                    act.wait_ge(S["qk_shift"], 2 * t.n + 2)
                    if c.exists:
                        act.wait_ge(S["pv_prod_p"], c.n + 1)
                        act.wait_ge(S["p_sum"], 2 * c.n + 2)
                    act.activation(p_sb[:, :], shifted[:, PD:PD + PP], ACT.Exp, scale=HD ** -0.5)\
                        .then_inc(S["p_ready_p"], 1)

            copy_q(Tile(0, 0))
            copy_k(Tile(0, 0))
            each_step(act, 0, NT + 3, 1, 4, step)

            act.wait_ge(S["tab_ready"], 1)
            fill_padding(act, 0, FILL_ACT, S["filled_act"])

            quads = n_quads(act)

            def copy_xT(n, par):
                act.wait_ge(S["cX_ps"], n + 1)
                if not (isinstance(n, int) and n < 2):
                    act.wait_ge(S["cgu_ps"], n - 1)
                act.activation(xtT[par][:, :], banks[2][:, :], ACT.Copy).then_inc(S["cX_copied"], 1)

            def copy_y(n, par, old):
                act.wait_ge(S["cy_ps"], n + 1)
                if old is not None:
                    act.wait_ge(y_scattered[par], old)
                act.activation(y_sb[par][:, :, :], banks[6 + par][:, :], ACT.Copy)\
                    .then_inc(S["cy_copied"], 1)

            def pairs(quad, par, has_prev, has_next):
                n = quad * 2 + par
                if has_next:
                    copy_xT(n + 1, 1 - par)
                act.wait_ge(S["cgu_ps"], n + 1)
                act.activation(cth[par][:, :, :],
                               banks[par][:, :].rearrange("p (j f) -> p j f", j=2)[:, :, 0:EI],
                               ACT.Tanh, scale=0.5).then_inc(S["cth_ready"], 1)
                if has_prev:
                    first = isinstance(n, int) and n < 3
                    copy_y(n - 1, 1 - par, None if first else (quad * 32 if par else quad * 32 - 32))

            copy_xT(0, 0)
            quads_with_ends(act, quads, pairs)
            copy_y(quads * 2 - 1, 1, quads * 32 - 32)

            with act.Fori(0, NT // DWAYS) as group:
                for par in range(DWAYS):
                    act.wait_ge(S["o2_ready"], group * DWAYS + (par + 1))
                    act.dma_start(out[bass.ds((group * DWAYS + par) * P, P), :], o2[par][:, :])\
                        .then_inc(stored[par], 16)
            for par in range(DWAYS):
                act.wait_ge(stored[par], 16 * (NT // DWAYS))

        @block.tensor
        def _(pe):
            pe.wait_ge(S["consts"], 15)
            pe.wait_ge(S["qkv_w"], 16)

            def mm(dst, lhsT, rhs, k, n):
                return pe.matmul(dst, lhsT, rhs, start=(k == 0), stop=(k == n - 1))

            def project_q(t):
                pe.wait_ge(xT_loaded[t.par], t.pair * 16 + 16)
                if t.since(2):
                    pe.wait_ge(S["qk_shift"], 2 * t.n - 2)
                for k in range(KC):
                    last = mm(qs_ps[t.par][:, 0:DM], xT_sb[t.par][:, k, :], wqkv_sb[:, k, 0:DM], k, KC)
                last.then_inc(S["q_ready"], 1)

            def project_kv(t, k):
                if k == 0 and t.since(1):
                    pe.wait_ge(S["v_copied"], t.n)
                last = mm(kv_ps[:, :], xT_sb[t.par][:, k, :], wqkv_sb[:, k, DM:3 * DM], k, KC)
                if k == KC - 1:
                    last.then_inc(S["kv_ready"], 1)

            def sum_products(dst, products, width):
                for i in range(HD):
                    last = mm(dst, ident[:, :], products[:, (i + 1) * PP - width:(i + 1) * PP], i, HD)
                return last

            def count_picks(b):
                groups = []
                if b.exists:
                    groups += [(before_b[:, :], onehot[b.par][:, k, :]) for k in range(TOPK)]
                if b.since(1):
                    groups += [(rest_b[:, :], onehot[1 - b.par][:, k, :]) for k in range(TOPK)]
                    groups += [(ident[:, :], ranks_sb[:, :])]
                for i, (rows, cols) in enumerate(groups):
                    last = mm(misc_ps[:, DM:DM + NE], rows, cols, i, len(groups))
                last.then_inc(S["rank_ready"], 1)

            def sum_pv(u):
                pe.wait_ge(S["pv_prod_p"], u.n + 1)
                pe.wait_ge(S["pv_prod_d"], u.n + 1)
                pe.wait_ge(S["p_sum"], 2 * u.n + 2)
                sum_products(att_ps[:, PVS:PVS + PP], prod_p, PP).then_inc(S["pv_sum_p"], 1)

            def last_tile(u):
                return isinstance(u.n, int) and u.n == NT - 1

            def step(t):
                c, a, b = t.ago(1), t.ago(2), t.ago(3)
                if a.exists and not last_tile(a):
                    sum_pv(a)
                if t.ago(-1).exists:
                    project_q(t.ago(-1))
                if a.exists or b.exists:
                    if b.exists:
                        pe.wait_ge(S["x1T_copied"], b.n + 1)
                if b.exists:
                    pe.wait_ge(S["hs_ready"], b.n + 1)
                    for k in range(SHI // P):
                        last = pe.transpose(tr_ps[:, (KC + k) * P:(KC + k + 1) * P],
                                            hs_sb[:, k * P:(k + 1) * P], ident[:, :])
                if a.exists:
                    pe.wait_ge(S["att_ready"], 2 * a.n + 2)
                    for k in range(KC):
                        last = pe.transpose(tr_ps[:, k * P:(k + 1) * P], o_sb[:, k * P:(k + 1) * P], ident[:, :])
                if a.exists or b.exists:
                    last.then_inc(S["ohT_ps"], 1)
                if t.ago(-1).exists:
                    project_kv(t.ago(-1), 0)
                if a.exists or b.exists:
                    pe.wait_ge(S["ohT_copied"], t.n - 1)
                if a.exists:
                    if a.since(1):
                        pe.wait_ge(S["eneg_ready"], a.n)
                    for k in range(KC):
                        last = mm(y_ps[:, 0:DM], ohT_sb[:, k, :], wfc_sb[:, k, :], k, KC)
                    last.then_inc(S["y_ready"], 1)
                if b.exists:
                    if b.since(1):
                        pe.wait_ge(S["rk"], b.n * RK - (RK - 1))
                    for k in range(SHI // P):
                        last = mm(misc_ps[:, 0:DM], ohT_sb[:, KC + k, :], wsd_sb[:, k, :], k, SHI // P)
                    last.then_inc(S["sd_ready"], 1)
                if t.ago(-1).exists:
                    project_kv(t.ago(-1), 1)
                if t.exists:
                    pe.wait_ge(S["qk_prod_p"], t.n + 1)
                    pe.wait_ge(S["qk_prod_d"], t.n + 1)
                    sum_products(qs_ps[t.par][:, QKS:QKS + TS], prod_q[t.par], TS).then_inc(S["qk_sum_p"], 1)
                if last_tile(c):
                    sum_pv(c)
                if a.exists:
                    pe.wait_ge(S["x1_ready"], a.n + 1)
                    for k in range(KC):
                        last = pe.transpose(tr_ps[:, k * P:(k + 1) * P], x1[a.par][:, k * P:(k + 1) * P],
                                            ident[:, :])
                    last.then_inc(S["x1T_ps"], 1)
                if b.exists:
                    pe.wait_ge(S["route"], b.n * ROUTE + ONEHOT)
                    pe.wait_ge(S["sx_ready"], b.n + 1)
                    count_picks(b)
                if a.exists:
                    pe.wait_ge(S["x1T_copied"], a.n + 1)
                    for k in range(KC):
                        last = mm(y_ps[:, DM:DM + NE], x1T_sb[:, k, :], wr_sb[:, k, :], k, KC)
                    last.then_inc(S["logits_ready"], 1)
                    if a.since(1):
                        pe.wait_ge(S["hs_ready"], a.n)
                    for k in range(KC):
                        last = mm(gu_ps[:, :], x1T_sb[:, k, :], wsgu_sb[:, k, :], k, KC)
                    last.then_inc(S["gu_ready"], 1)

            project_q(Tile(0, 0))
            project_kv(Tile(0, 0), 0)
            project_kv(Tile(0, 0), 1)
            pe.wait_ge(S["small_w"], NSMALL)
            each_step(pe, 0, NT + 3, 1, 4, step)

            pe.wait_ge(S["rk"], NT * RK)
            count_picks(Tile(NT // 2, 0))
            pe.wait_ge(S["b"], BSTEPS)
            for c in range(4):
                last = pe.transpose(tr_ps[0:1, c * P:(c + 1) * P], slot_row[:, c:c + 1], ident[:, :])
            last.then_inc(S["tabT"], 1)

            pe.wait_ge(S["big_w"], 16 * (NE + 2))
            quads = n_quads(pe)

            def transposes(n, par, quad):
                pe.wait_ge(xt_loaded[par], quad * 32 + 32)
                if not (isinstance(n, int) and n < 1):
                    pe.wait_ge(S["cX_copied"], n)
                for j in range(2):
                    for k in range(KC):
                        c = (j * KC + k) * P
                        last = pe.transpose(banks[2][:, c:c + P], xt[par][:, j, k * P:(k + 1) * P], ident[:, :])
                last.then_inc(S["cX_ps"], 1)

            def quad_experts(quad):
                return pe.value_load(tab[0:1, bass.ds(quad + SLOTS, 1)], min_val=0, max_val=NE ** (QUAD + 2) - 1)

            def expert(word, slot):
                return (word // NE ** slot) % NE

            def pairs(quad, par, has_prev, has_next):
                n = quad * 2 + par
                if has_next:
                    transposes(n + 1, 1 - par, quad if par == 0 else quad + 1)
                if par == 0:
                    word[0] = quad_experts(quad)
                for j in range(2):
                    woff = expert(word[0], 2 * par + j) * (KC * 2 * EI)
                    if j == 0:
                        pe.wait_ge(S["cX_copied"], n + 1)
                        if not (isinstance(n, int) and n < 2):
                            pe.wait_ge(S["ch_ready"], 2 * n - 2)
                    for k in range(KC):
                        c = (j * KC + k) * P
                        last = mm(banks[par][:, j * 2 * EI:(j + 1) * 2 * EI], xtT[par][:, c:c + P],
                                  wgu_sb[:, bass.ds(woff + k * 2 * EI, 2 * EI)], k, KC)
                    if j == 0 and has_prev:
                        transpose_h(n - 1)
                last.then_inc(S["cgu_ps"], 1)
                if has_prev:
                    down(n - 1, 1 - par, 0 if par else QUAD)

            def transpose_h(n):
                pe.wait_ge(S["ch_ready"], 2 * n + 2)
                if not (isinstance(n, int) and n < 1):
                    pe.wait_ge(S["chT_copied"], n)
                for j in range(2):
                    last = pe.transpose(banks[3][:, j * P:(j + 1) * P], ch[:, j, :], ident[:, :])
                last.then_inc(S["chT_ps"], 1)

            word = [None]

            def down(n, par, slot):
                pe.wait_ge(S["chT_copied"], n + 1)
                if not (isinstance(n, int) and n < 2):
                    pe.wait_ge(S["cy_copied"], n - 1)
                for j in range(2):
                    last = mm(banks[6 + par][:, j * DM:(j + 1) * DM], chT[:, j * P:(j + 1) * P],
                              wd_sb[:, bass.ds(expert(word[0], slot + j) * DM, DM)], 0, 1)
                last.then_inc(S["cy_ps"], 1)

            transposes(0, 0, 0)
            quads_with_ends(pe, quads, pairs)
            transpose_h(quads * 2 - 1)
            down(quads * 2 - 1, 1, 2)

            def sum_rows(t):
                pe.wait_ge(S["d_a"], t.n + 1)
                if t.since(DWAYS):
                    pe.wait_ge(S["o2_ready"], t.n - (DWAYS - 1))
                for i in range(2):
                    mm(banks[t.par][:, 0:DM], ident[:, :], z2[t.par][:, i, :], i, 3)
                mm(banks[t.par][:, 0:DM], ident[:, :], sx[:, bass.ds(t.n * DM, DM)], 2, 3)\
                    .then_inc(S["d_ps"], 1)

            each_step(pe, 0, NT - 1, 0, 0, sum_rows, DWAYS, 1)

        @block.vector
        def _(dve):
            dve.memset(gscore[:, :], -3.0e38).then_inc(S["cast"], 1)
            for i in range(2):
                dve.memset(stage[i][:, :, WT + 1:ROW], 0.0).then_inc(S["cast"], 1)
            dve.memset(ones_e[:, :], 1.0).then_inc(S["cast"], 1)
            dve.wait_ge(S["consts"], 15)
            dve.wait_ge(S["small_w"], NSMALL)
            dve.wait_ge(S["cast"], 4)
            def step(t):
                c, a, b, d = t.ago(1), t.ago(2), t.ago(3), t.ago(4)
                done = [0]

                def at(ins):
                    done[0] += 1
                    return ins.then_inc(S["route"], 1)

                def after(apart=False):
                    if apart:
                        wait_apart(dve, S["route"], b.n * ROUTE + done[0])
                    else:
                        dve.wait_ge(S["route"], b.n * ROUTE + done[0])

                def qk_products(h0, h1):
                    n = h1 - h0
                    ins = dve.tensor_tensor(
                        prod_d[:, h0 * HW:h1 * HW].rearrange("p (h g d) -> p h g d", h=n, g=NH),
                        qs_ps[t.par][:, h0 * HD:h1 * HD].rearrange("p (h o d) -> p h o d", h=n, o=1)
                        .broadcast_to([P, n, NH, HD]),
                        k_sb[t.par][:, :].rearrange("p (o g d) -> p o g d", o=1, g=NH)
                        .broadcast_to([P, n, NH, HD]), ALU.mult)
                    if h1 == NDH:
                        ins.then_inc(S["qk_prod_d"], 1)

                def pv_products(h0, h1):
                    n = h1 - h0
                    ins = dve.tensor_tensor(
                        prod_d[:, h0 * HW:h1 * HW].rearrange("p (h d g) -> p h d g", h=n, d=HD),
                        att_ps[:, h0 * NH:h1 * NH].rearrange("p (h o g) -> p h o g", h=n, o=1)
                        .broadcast_to([P, n, HD, NH]),
                        v_sb[c.par][:, :].rearrange("p (o d g) -> p o d g", o=1, g=NH)
                        .broadcast_to([P, n, HD, NH]), ALU.mult)
                    if h1 == NDH:
                        ins.then_inc(S["pv_prod_d"], 1)

                if t.exists:
                    dve.wait_ge(S["q_ready"], t.n + 1)
                    dve.wait_ge(S["k_copied"], t.n + 1)
                    qk_products(0, NDH // 2)
                if d.exists:
                    dve.wait_ge(S["rank_ready"], d.n + 1)
                    dve.tensor_copy(ranks_sb[:, :], misc_ps[:, DM:DM + NE]).then_inc(S["rk"], 1)
                if b.exists:
                    dve.wait_ge(S["eneg_ready"], b.n + 1)
                    at(dve.tensor_scalar(eneg1[:, :], eneg[:, :], 1.0, None, ALU.add))
                if d.exists:
                    dve.wait_ge(S["rk"], d.n * RK + 1)
                    dve.tensor_tensor(rsel[:, :, :], onehot[d.par][:, :, :],
                                      ranks_sb[:, :].unsqueeze(1).broadcast_to([P, TOPK, NE]),
                                      ALU.mult).then_inc(S["rk"], 1)
                if b.exists:
                    dve.wait_ge(S["th_ready"], b.n + 1)
                    dve.scalar_tensor_tensor(out=gth_sb[:, :], in0=th_sb[:, :], scalar=1.0,
                                             in1=gu_ps[:, 0:SHI], op0=ALU.add, op1=ALU.mult)\
                        .then_inc(S["gth_ready"], 1)
                if d.exists:
                    dve.wait_ge(S["rk"], d.n * RK + 2)
                    dve.tensor_reduce(rank[:, :], rsel[:, :, :], AX, ALU.add).then_inc(S["rk"], 1)
                if b.exists:
                    after()
                    at(dve.reciprocal(sig[:, :], eneg1[:, :]))
                if d.exists:
                    dve.wait_ge(S["rk"], d.n * RK + 3)
                    if d.since(2):
                        dve.wait_ge(scattered[d.par], d.pair * (16 * TOPK))
                    dve.wait_ge(S["route"], (d.n + 1) * ROUTE)
                    dve.wait_ge(S["staged"], d.n + 1)
                    dve.scalar_tensor_tensor(out=pos[d.par][:, :], in0=bidx[:, 0:TOPK], scalar=float(REGION),
                                             in1=rank[:, :], op0=ALU.mult, op1=ALU.add)\
                        .then_inc(S["pos_ready"], 1)
                if b.exists:
                    dve.wait_ge(S["gth_ready"], b.n + 1)
                    if b.since(1):
                        dve.wait_ge(S["ohT_ps"], t.n - 2)
                    dve.scalar_tensor_tensor(out=hs_sb[:, :], in0=gth_sb[:, :], scalar=0.5,
                                             in1=gu_ps[:, SHI:2 * SHI], op0=ALU.mult, op1=ALU.mult)\
                        .then_inc(S["hs_ready"], 1)
                if a.exists:
                    dve.wait_ge(S["pv_sum_d"], a.n + 1)
                    dve.wait_ge(S["p_rec"], a.n + 1)
                    if a.since(1):
                        dve.wait_ge(S["ohT_ps"], a.n)
                    dve.tensor_tensor(o_sb[:, 0:NDH * HD].rearrange("p (h d) -> p h d", h=NDH),
                                      att[:, :].rearrange("p (h d) -> p h d", h=NDH),
                                      prec[:, 0:NDH].unsqueeze(2).broadcast_to([P, NDH, HD]), ALU.mult)\
                        .then_inc(S["att_ready"], 1)
                    dve.wait_ge(S["pv_sum_p"], a.n + 1)
                    dve.tensor_tensor(o_sb[:, NDH * HD:DM].rearrange("p (h d) -> p h d", h=NPH),
                                      att_ps[:, PVS:PVS + PP].rearrange("p (h d) -> p h d", h=NPH),
                                      prec[:, NDH:NH].unsqueeze(2).broadcast_to([P, NPH, HD]), ALU.mult)\
                        .then_inc(S["att_ready"], 1)
                if t.exists:
                    qk_products(NDH // 2, NDH)
                if b.exists:
                    after()
                    at(dve.tensor_tensor(sfc[:, :], sig[:, :], bias_sb[:, :], ALU.add))
                if b.exists:
                    after(apart=True)
                    for g in range(NGROUP):
                        at(dve.max(gtop[:, g, :], sfc[:, g * GSZ:(g + 1) * GSZ]))
                if t.exists:
                    dve.wait_ge(S["qk_prod_d"], t.n + 1)
                    dve.tensor_reduce(scores[:, 0:PD], prod_d.rearrange("p (s d) -> p s d", d=HD), AX, ALU.add)\
                        .then_inc(S["qk_sum_d"], 1)
                if a.exists:
                    dve.wait_ge(S["y_ready"], a.n + 1)
                    dve.wait_ge(x_loaded[a.par], a.pair * 16 + 16)
                    if a.since(1):
                        dve.wait_ge(S["x1_ready"], a.n)
                    dve.tensor_tensor(res[:, :], x_sb[a.par][:, :], y_ps[:, 0:DM], ALU.add)\
                        .then_inc(S["res_ready"], 1)
                if b.exists:
                    after()
                    at(dve.tensor_tensor(gscore[:, 0:NGROUP], gtop[:, :, 0], gtop[:, :, 1], ALU.add))
                if b.exists:
                    after(apart=True)
                    at(dve.max(gbest[:, :], gscore[:, :]))
                if b.exists:
                    after(apart=True)
                    at(dve.max_index(gidx[:, :], gbest[:, :], gscore[:, :]))
                if c.exists:
                    dve.wait_ge(S["p_ready_d"], c.n + 1)
                    dve.tensor_reduce(psum_row[:, 0:NDH], att_ps[:, 0:PD].rearrange("p (h g) -> p h g", h=NDH),
                                      AX, ALU.add).then_inc(S["p_sum"], 1)
                if b.exists:
                    after()
                    at(dve.tensor_tensor(gmask2[:, :, :],
                                         iota_e[:, 0:NGROUP].unsqueeze(1).broadcast_to([P, 2, NGROUP]),
                                         gidx[:, 0:2].unsqueeze(2).broadcast_to([P, 2, NGROUP]), ALU.is_equal))
                if c.exists:
                    dve.wait_ge(S["p_ready_p"], c.n + 1)
                    dve.tensor_reduce(psum_row[:, NDH:NH], p_sb[:, :].rearrange("p (h g) -> p h g", h=NPH),
                                      AX, ALU.add).then_inc(S["p_sum"], 1)
                if b.exists:
                    after()
                    at(dve.tensor_tensor(gmask[:, :], gmask2[:, 0, :], gmask2[:, 1, :], ALU.add))
                if c.exists:
                    dve.wait_ge(S["p_sum"], 2 * c.n + 2)
                    dve.reciprocal(prec[:, :], psum_row[:, :]).then_inc(S["p_rec"], 1)
                if b.exists:
                    after()
                    at(dve.tensor_tensor(masked[:, :].rearrange("p (g e) -> p g e", g=NGROUP),
                                         sfc[:, :].rearrange("p (g e) -> p g e", g=NGROUP),
                                         gmask[:, :].unsqueeze(2).broadcast_to([P, NGROUP, GSZ]), ALU.mult))
                if b.exists:
                    after(apart=True)
                    at(dve.max(best[:, :], masked[:, :]))
                if c.exists:
                    pv_products(0, NDH // 2)
                if b.exists:
                    after(apart=True)
                    at(dve.max_index(bidx[:, :], best[:, :], masked[:, :]))
                if c.exists:
                    pv_products(NDH // 2, NDH)
                if b.exists:
                    after()
                    if b.since(2):
                        dve.wait_ge(S["rank_ready"], b.n)
                    at(dve.tensor_tensor(onehot[b.par][:, :, :],
                                         iota_e[:, :].unsqueeze(1).broadcast_to([P, TOPK, NE]),
                                         bidx[:, 0:TOPK].unsqueeze(2).broadcast_to([P, TOPK, NE]), ALU.is_equal))
                    assert done[0] == ONEHOT
                    dve.wait_ge(S["sd_ready"], b.n + 1)
                    dve.wait_ge(S["x1_ready"], b.n + 1)
                    dve.tensor_tensor(sx[:, bass.ds(b.n * DM, DM)], x1[b.par][:, :], misc_ps[:, 0:DM], ALU.add)\
                        .then_inc(S["sx_ready"], 1)
                    after()
                    at(dve.tensor_tensor(wsel[:, :, :], onehot[b.par][:, :, :],
                                         sig[:, :].unsqueeze(1).broadcast_to([P, TOPK, NE]), ALU.mult))
                if b.exists:
                    after()
                    at(dve.tensor_reduce(w4[:, :], wsel[:, :, :], AX, ALU.add))
                if t.exists:
                    dve.wait_ge(S["qk_prod_p"], t.n + 1)
                    dve.tensor_reduce(scores[:, PD:VS],
                                      prod_q[t.par].rearrange("p (d s) -> p s d", d=HD)[:, 0:NH, :], AX, ALU.add)\
                        .then_inc(S["qk_sum_x"], 1)
                if c.exists:
                    dve.wait_ge(S["pv_prod_d"], c.n + 1)
                    dve.tensor_reduce(att[:, :], prod_d.rearrange("p (s g) -> p s g", g=NH), AX, ALU.add)\
                        .then_inc(S["pv_sum_d"], 1)
                if b.exists:
                    after()
                    at(dve.tensor_reduce(wsum[:, :], w4[:, :], AX, ALU.add))
                if t.exists:
                    dve.wait_ge(S["qk_sum_d"], t.n + 1)
                    dve.wait_ge(S["qk_sum_x"], t.n + 1)
                    sc_d = scores[:, :].rearrange("p (h g) -> p h g", h=NVS)
                    dve.tensor_reduce(smax[:, 0:NVS], sc_d, AX, ALU.max).then_inc(S["qk_max"], 1)
                if b.exists:
                    after()
                    at(dve.tensor_scalar(wsum1[:, :], wsum[:, :], 1e-20, None, ALU.add))
                if t.exists:
                    dve.wait_ge(S["qk_sum_p"], t.n + 1)
                    sc_p = qs_ps[t.par][:, QKS:QKS + TS].rearrange("p (h g) -> p h g", h=NTS)
                    dve.tensor_reduce(smax[:, NVS:NH], sc_p, AX, ALU.max).then_inc(S["qk_max"], 1)
                if b.exists:
                    after()
                    at(dve.reciprocal(wrec[:, :], wsum1[:, :]))
                if t.exists:
                    dve.wait_ge(S["qk_max"], 2 * t.n + 2)
                    if c.exists:
                        dve.wait_ge(S["p_ready_p"], c.n + 1)
                        dve.wait_ge(S["p_ready_d"], c.n + 1)
                    dve.tensor_tensor(shifted[:, 0:VS].rearrange("p (h g) -> p h g", h=NVS), sc_d,
                                      smax[:, 0:NVS].unsqueeze(2).broadcast_to([P, NVS, NH]), ALU.subtract)\
                        .then_inc(S["qk_shift"], 1)
                    dve.tensor_tensor(shifted[:, VS:VS + TS].rearrange("p (h g) -> p h g", h=NTS), sc_p,
                                      smax[:, NVS:NH].unsqueeze(2).broadcast_to([P, NTS, NH]), ALU.subtract)\
                        .then_inc(S["qk_shift"], 1)
                if b.exists:
                    after()
                    if b.since(2):
                        dve.wait_ge(scattered[b.par], b.pair * (16 * TOPK))
                    at(dve.tensor_scalar(stage[b.par][:, :, WT], w4[:, :], wrec[:, 0:1], SCALE / 2,
                                         ALU.mult, ALU.mult))
                    assert done[0] == ROUTE

            each_step(dve, 0, NT + 3, 1, 4, step)

            steps = [0]

            def at(ins):
                steps[0] += 1
                return ins.then_inc(S["b"], 1)

            def after():
                dve.wait_ge(S["b"], steps[0])

            dve.wait_ge(S["rank_ready"], NT + 1)
            at(dve.tensor_scalar(cnt_u[:, :], misc_ps[:, DM:DM + NE], float(P - 1), None, ALU.add))
            after()
            at(dve.tensor_scalar(ntile_u[:, :], cnt_u[:, :], 7, None, ALU.logical_shift_right))
            after()
            at(dve.tensor_copy(ntile[:, :], ntile_u[:, :]))
            after()
            at(dve.tensor_tensor_scan(tend[:, :], ones_e[:, :], ntile[:, :], 0.0, ALU.mult, ALU.add))
            after()
            for c in range(2):
                at(dve.tensor_scalar(past[:, c, :], tend[:, :], slot_col[:, c:c + 1], None, ALU.is_le))
            after()
            at(dve.tensor_reduce(slot_e[:, :], past[:, :, :], AX, ALU.add))
            at(dve.tensor_tensor(pend[:, :, :], past[:, :, :],
                                 tend[:, :].unsqueeze(1).broadcast_to([P, 2, NE]), ALU.mult))
            after()
            at(dve.tensor_reduce(slot_first[:, :], pend[:, :, :], AX, ALU.max))
            after()
            at(dve.tensor_tensor(slot_k[:, :], slot_col[:, :], slot_first[:, :], ALU.subtract))
            after()
            at(dve.tensor_scalar(slot_k[:, :], slot_k[:, :], float(P), None, ALU.mult))
            after()
            at(dve.scalar_tensor_tensor(out=slot_row[:, 0:2], in0=slot_e[:, :], scalar=float(REGION),
                                        in1=slot_k[:, :], op0=ALU.mult, op1=ALU.add))
            at(dve.tensor_scalar(slot_row[:, 2:4], slot_e[:, :], float(NE - 1), None, ALU.min))
            assert steps[0] == BSTEPS
            dve.wait_ge(S["tabT"], 1)
            at(dve.tensor_copy(tab[0:1, 0:SLOTS], tr_ps[0:1, 0:SLOTS]))
            experts = tr_ps[0:1, SLOTS:2 * SLOTS].rearrange("p (q j) -> p q j", j=QUAD)
            at(dve.tensor_copy(pack[0][:, :], experts[:, :, QUAD - 1]))
            at(dve.tensor_tensor(tab[0:1, PADS:PADS + NE], region0[0:1, :], misc_ps[0:1, DM:DM + NE], ALU.add))
            at(dve.tensor_scalar(quadf[:, :], tend[:, NE - 1:NE], float(QUAD - 1 - 2 * QUAD), None, ALU.add))
            after()
            at(dve.tensor_scalar(tab[0:1, QUADS:QUADS + 1].bitcast(U32), quadf[0:1, :], 2, None,
                                 ALU.logical_shift_right))
            for j in (2, 1, 0):
                after()
                to = packed[:, :] if j == 0 else pack[(j + 1) % 2][:, :]
                at(dve.scalar_tensor_tensor(out=to, in0=pack[j % 2][:, :], scalar=float(NE),
                                            in1=experts[:, :, j], op0=ALU.mult, op1=ALU.add))
            after()
            tab_u = tab[0:1, :].bitcast(U32)
            at(dve.tensor_scalar(before[:, 1:], packed[:, 0:SLOTS // QUAD - 1], 2 * EBITS, QUAD * EBITS,
                                 ALU.logical_shift_right, ALU.logical_shift_left))
            at(dve.tensor_copy(tab_u[:, SLOTS:SLOTS + 1], packed[:, 0:1]))
            after()
            at(dve.tensor_tensor(tab_u[:, SLOTS + 1:PADS], before[:, 1:], packed[:, 1:], ALU.bitwise_or))
            after()
            dve.memset(quadf[:, :], 0.0).then_inc(S["tab_ready"], 1)

            quads = n_quads(dve)

            def copy_meta(n, par, quad):
                dve.wait_ge(xt_loaded[par], quad * 32 + 32)
                if not (isinstance(n, int) and n < 2):
                    dve.wait_ge(S["ids_ready"], n - 1)
                dve.tensor_copy(meta[par][:, :, :], xt[par][:, :, ID:ID + 2]).then_inc(S["cmeta"], 1)

            def pairs(quad, par, has_prev, has_next):
                n = quad * 2 + par
                if has_next:
                    copy_meta(n + 1, 1 - par, quad + par)
                g_u = banks[par][:, :].rearrange("p (j f) -> p j f", j=2)
                dve.wait_ge(S["cth_ready"], n + 1)
                dve.scalar_tensor_tensor(out=cgth[:, :, :], in0=cth[par][:, :, :], scalar=1.0,
                                         in1=g_u[:, :, 0:EI], op0=ALU.add, op1=ALU.mult)\
                    .then_inc(S["cgth_ready"], 1)
                dve.wait_ge(S["cgth_ready"], n + 1)
                dve.wait_ge(S["cmeta"], n + 1)
                if has_prev:
                    dve.wait_ge(S["chT_ps"], n)
                for j in range(2):
                    dve.scalar_tensor_tensor(out=ch[:, j, :], in0=cgth[:, j, :], scalar=meta[par][:, j, 1:2],
                                             in1=g_u[:, j, EI:2 * EI], op0=ALU.mult, op1=ALU.mult)\
                        .then_inc(S["ch_ready"], 1)
                dve.wait_ge(S["chT_ps"], n + 1)
                if has_prev:
                    dve.wait_ge(S["cy_ps"], n)
                dve.tensor_copy(chT[:, :], banks[3][:, 0:2 * P]).then_inc(S["chT_copied"], 1)
                if not (isinstance(n, int) and n < 2):
                    dve.wait_ge(y_scattered[par], quad * 32)
                dve.tensor_copy(ids[par][:, :], meta[par][:, :, 0]).then_inc(S["ids_ready"], 1)

            copy_meta(0, 0, 0)
            quads_with_ends(dve, quads, pairs)

            def dstep(t):
                a, b = t.ago(1), t.ago(2)
                if t.exists:
                    dve.wait_ge(z_loaded[t.par], t.pair * 16 + 16)
                    if t.since(DWAYS):
                        dve.wait_ge(S["d_ps"], t.n - (DWAYS - 1))
                    dve.tensor_tensor(z2[t.par][:, :, :], zt[t.par][:, 0:2, :], zt[t.par][:, 2:4, :], ALU.add)\
                        .then_inc(S["d_a"], 1)
                if b.exists:
                    dve.wait_ge(S["drstd_ready"], b.n + 1)
                    if b.since(DWAYS):
                        dve.wait_ge(stored[b.par], b.pair * 16)
                    dve.tensor_scalar(o2[b.par][:, :], banks[b.par][:, 0:DM], mv[b.par][:, 0:1],
                                      rstd[b.par][:, 0:1], ALU.subtract, ALU.mult)\
                        .then_inc(S["o2_ready"], 1)
                if a.exists:
                    dve.wait_ge(S["d_ps"], a.n + 1)
                    dve.bn_stats(stats[:, :], banks[a.par][:, 0:DM]).then_inc(S["dst_ready"], 1)
                    wait_apart(dve, S["dst_ready"], a.n + 1)
                    dve.bn_aggr(mv[a.par][:, :], stats[:, :]).then_inc(S["dmv_ready"], 1)
                    dve.wait_ge(S["dmv_ready"], a.n + 1)
                    dve.tensor_scalar(veps[a.par][:, :], mv[a.par][:, 1:2], EPS, None, ALU.add)\
                        .then_inc(S["dveps_ready"], 1)

            each_step(dve, 0, NT + 1, 0, 2, dstep, DWAYS, 1)


ONEHOT = 16
ROUTE = 22
RK = 3
BSTEPS = 13


def kernel(L0_attn_x, L0_attn_Wq, L0_attn_Wk, L0_attn_Wv, L0_attn_Wfc, L0_ffn_router_weight,
           L0_ffn_router_bias, L0_ffn_gate_w, L0_ffn_up_w, L0_ffn_down_w, L0_ffn_shared_gate_w,
           L0_ffn_shared_up_w, L0_ffn_shared_down_w):
    import numpy as np
    import concourse.bacc as bacc
    from concourse.bass_utils import run_bass_kernel_spmd

    def arr(a):
        return np.asarray(a)

    def chunked(w):
        w = arr(w)
        return np.ascontiguousarray(w.reshape(w.shape[0], -1, P).transpose(2, 1, 0))

    x = arr(L0_attn_x).reshape(NTOK, DM)
    wv = arr(L0_attn_Wv).reshape(NH, HD, DM).transpose(1, 0, 2).reshape(DM, DM)
    gate = arr(L0_ffn_gate_w).reshape(NE, EI, KC, P)
    up = arr(L0_ffn_up_w).reshape(NE, EI, KC, P)
    ins = {
        "xT": x.reshape(NT, P, KC, P).transpose(0, 3, 2, 1).reshape(NTOK, DM),
        "x": x,
        "wqkv": chunked(np.concatenate([arr(L0_attn_Wq), arr(L0_attn_Wk), wv], axis=0)),
        "wfc": chunked(L0_attn_Wfc),
        "wr": chunked(L0_ffn_router_weight),
        "rbias": np.broadcast_to(arr(L0_ffn_router_bias)[None, :], (P, NE)),
        "wsgu": chunked(np.concatenate([arr(L0_ffn_shared_gate_w), arr(L0_ffn_shared_up_w)], axis=0)),
        "wsd": chunked(L0_ffn_shared_down_w),
        "wgu": np.concatenate([gate, up], axis=1).transpose(3, 0, 2, 1).reshape(P, -1),
        "wd": arr(L0_ffn_down_w).transpose(2, 0, 1).reshape(P, -1),
    }
    nc = bacc.Bacc("TRN2", target_bir_lowering=False, num_devices=1)
    arrays, args = {}, []
    for name, a in ins.items():
        a = np.ascontiguousarray(a)
        arrays[f"in_{name}"] = a
        args.append(nc.dram_tensor(f"in_{name}", a.shape, mybir.dt.from_np(a.dtype), kind="ExternalInput").ap())
    args.append(nc.dram_tensor("out_0", (NTOK, DM), F32, kind="ExternalOutput").ap())
    build(nc, *args)
    r = run_bass_kernel_spmd(nc, [arrays], core_ids=[0])
    return r.results[0]["out_0"].reshape(4, NTOK // 4, DM)
```
